# Optimizing a Trainium2 kernel written in Bass

```python
import numpy as np
import jax
import jax.numpy as jnp

def _softmax(x, axis=-1):
    return jax.nn.softmax(x, axis=axis)

def _gelu(x):
    return jax.nn.gelu(x, approximate=True)

def _silu(x):
    return jax.nn.silu(x)

def _sigmoid(x):
    return jax.nn.sigmoid(x)

def _layernorm(x, axis=-1, eps=1e-05):
    m = jnp.mean(x, axis=axis, keepdims=True)
    v = jnp.var(x, axis=axis, keepdims=True)
    return (x - m) / jnp.sqrt(v + eps)

def _scatter_add(tgt, idx, src, axis=0):
    return tgt.at[idx].add(src)

def _segment_sum(src, seg, n):
    return jax.ops.segment_sum(src, seg, n)
kernel_name = 'mk_audio_tower_d2_tok_audfeat512_r4_db443b'

def setup_inputs(seed: int=0):
    np.random.seed(seed)
    _w = jnp.asarray

    def _rec_inputs():
        import jax
        import jax.numpy as jnp
        _rk = jax.random.key(seed)
        x = -7.10856e-05 + 0.999911 * jax.random.normal(jax.random.fold_in(_rk, 1), (8, 4096, 128), jnp.float32)
        return x
    x = _rec_inputs()

    def _L0_tok_setup():
        import jax, jax.numpy as jnp
        import numpy as np
        BLOCK = 128
        TOP_K = 16
        key = jax.random.key(seed)
        k1, k2 = jax.random.split(key)
        B, S, D = (8, 4096, 128)
        x = jax.random.normal(k1, (B, S, D), dtype=jnp.float32)
        W = jax.random.normal(k2, (1, D), dtype=jnp.float32) * (1.0 / np.sqrt(D))
        b = jnp.zeros((1,), dtype=jnp.float32)
        return {'x': x, 'W': W, 'b': b}
    _L0_tok_all = _L0_tok_setup()
    _L0_tok_in = {k: v for k, v in _L0_tok_all.items() if k in ('W', 'b')}
    del _L0_tok_all

    def _L0_attn_setup():
        import jax, jax.numpy as jnp
        import numpy as np
        import math
        N_HEADS = 4
        EPS = 1e-06

        def rmsnorm(x, w, eps=EPS):
            xf = x.astype(jnp.float32)
            rms = jax.lax.rsqrt(jnp.mean(xf * xf, axis=-1, keepdims=True) + eps)
            return w * (xf * rms)

        def rope(x):
            L, d = (x.shape[1], x.shape[-1])
            inv_freq = 1.0 / 10000.0 ** (jnp.arange(0, d, 2, dtype=jnp.float32) / d)
            t = jnp.arange(L, dtype=jnp.float32)
            freqs = jnp.outer(t, inv_freq)
            emb = jnp.concatenate([freqs, freqs], axis=-1)
            cos = jnp.cos(emb)[None, :, None, :]
            sin = jnp.sin(emb)[None, :, None, :]
            x1, x2 = jnp.split(x, 2, axis=-1)
            x_rot = jnp.concatenate([-x2, x1], axis=-1)
            return x * cos + x_rot * sin
        key = jax.random.key(seed)
        ks = jax.random.split(key, 8)
        B, L, D, LAT, H = (2, 128, 128, 64, N_HEADS)
        dh = D // H
        s = 0.02
        return {'x': jax.random.normal(ks[0], (B, L, D), jnp.float32), 'ln_w': jnp.ones((D,), jnp.float32), 'Wc': jax.random.normal(ks[1], (D, LAT), jnp.float32) * s, 'Wqkv': jax.random.normal(ks[2], (LAT, 3 * D), jnp.float32) * s, 'Wreso': jax.random.normal(ks[3], (LAT, 4 * H), jnp.float32) * s, 'qn_w': jnp.ones((dh,), jnp.float32), 'kn_w': jnp.ones((dh,), jnp.float32), 'Wg': jax.random.normal(ks[4], (LAT, D), jnp.float32) * s, 'head_decay': jnp.linspace(-3.0, 1.0, H), 'temperature': jnp.ones((1,), jnp.float32) * 0.5, 'Wp': jax.random.normal(ks[5], (D, D), jnp.float32) * s, 'mem_w': jnp.ones((D,), jnp.float32)}
    _L0_attn_all = _L0_attn_setup()
    _L0_attn_in = {k: v for k, v in _L0_attn_all.items() if k in ('ln_w', 'Wc', 'Wqkv', 'Wreso', 'qn_w', 'kn_w', 'Wg', 'head_decay', 'temperature', 'Wp', 'mem_w')}
    del _L0_attn_all

    def _L0_ffn_setup():
        import jax, jax.numpy as jnp
        import numpy as np
        B, S, D = (8, 1024, 128)
        H = 512
        O = 128
        E = 8
        TOP_K = 1
        key = jax.random.key(seed)
        ks = jax.random.split(key, 8)
        sc = 0.02
        return {'x': jax.random.normal(ks[0], (B, S, D), dtype=jnp.float32), 'Wr': jax.random.normal(ks[1], (D, E), dtype=jnp.float32) * sc, 'br': jnp.zeros((E,), dtype=jnp.float32), 'W1': jax.random.normal(ks[2], (E, D, H), dtype=jnp.float32) * sc, 'b1': jnp.zeros((E, H), dtype=jnp.float32), 'W2': jax.random.normal(ks[3], (E, H, O), dtype=jnp.float32) * sc, 'b2': jnp.zeros((E, O), dtype=jnp.float32)}
    _L0_ffn_all = _L0_ffn_setup()
    _L0_ffn_in = {k: v for k, v in _L0_ffn_all.items() if k in ('Wr', 'br', 'W1', 'b1', 'W2', 'b2')}
    del _L0_ffn_all

    def _L1_attn_setup():
        import math
        import jax, jax.numpy as jnp
        import numpy as np
        EMBED = 128
        HEADS = 2
        HEAD_DIM = EMBED // HEADS
        key = jax.random.key(seed)
        ks = jax.random.split(key, 10)
        s = 1.0 / math.sqrt(EMBED)
        return {'text_embeds': jax.random.normal(ks[0], (64, 32, EMBED), jnp.float32), 'video_embeds': jax.random.normal(ks[1], (128, 64, EMBED), jnp.float32), 'Wq': jax.random.normal(ks[2], (EMBED, EMBED), jnp.float32) * s, 'bq': jnp.zeros((EMBED,), jnp.float32), 'Wk': jax.random.normal(ks[3], (EMBED, EMBED), jnp.float32) * s, 'bk': jnp.zeros((EMBED,), jnp.float32), 'Wv': jax.random.normal(ks[4], (EMBED, EMBED), jnp.float32) * s, 'bv': jnp.zeros((EMBED,), jnp.float32), 'Wo': jax.random.normal(ks[5], (EMBED, EMBED), jnp.float32) * s, 'bo': jnp.zeros((EMBED,), jnp.float32)}
    _L1_attn_all = _L1_attn_setup()
    _L1_attn_in = {k: v for k, v in _L1_attn_all.items() if k in ('video_embeds', 'Wq', 'bq', 'Wk', 'bk', 'Wv', 'bv', 'Wo', 'bo')}
    del _L1_attn_all

    def _L1_ffn_setup():
        import jax, jax.numpy as jnp
        import numpy as np
        K = 2
        EPS = 1e-06

        def _layernorm(x, gamma, beta):
            mu = jnp.mean(x, axis=-1, keepdims=True)
            var = jnp.mean(jnp.square(x - mu), axis=-1, keepdims=True)
            return (x - mu) * jax.lax.rsqrt(var + EPS) * gamma + beta
        key = jax.random.key(seed)
        ks = jax.random.split(key, 5)
        B, S, D, F, E = (8, 512, 128, 512, 8)
        x = jax.random.normal(ks[0], (B, S, D), dtype=jnp.float32)
        router_w = jax.random.normal(ks[1], (D, E), dtype=jnp.float32) * 0.02
        w1 = jax.random.normal(ks[2], (E, D, F), dtype=jnp.float32) * 0.02
        b1 = jnp.zeros((E, F), dtype=jnp.float32)
        w2 = jax.random.normal(ks[3], (E, F, D), dtype=jnp.float32) * 0.02
        b2 = jnp.zeros((E, D), dtype=jnp.float32)
        gamma = jnp.ones((E, D), dtype=jnp.float32)
        beta = jnp.zeros((E, D), dtype=jnp.float32)
        return {'x': x, 'router_w': router_w, 'w1': w1, 'b1': b1, 'w2': w2, 'b2': b2, 'gamma': gamma, 'beta': beta}
    _L1_ffn_all = _L1_ffn_setup()
    _L1_ffn_in = {k: v for k, v in _L1_ffn_all.items() if k in ('router_w', 'w1', 'b1', 'w2', 'b2', 'gamma', 'beta')}
    del _L1_ffn_all
    return {'x': x, 'L0_tok_W': _L0_tok_in['W'], 'L0_tok_b': _L0_tok_in['b'], 'L0_attn_ln_w': _L0_attn_in['ln_w'], 'L0_attn_Wc': _L0_attn_in['Wc'], 'L0_attn_Wqkv': _L0_attn_in['Wqkv'], 'L0_attn_Wreso': _L0_attn_in['Wreso'], 'L0_attn_qn_w': _L0_attn_in['qn_w'], 'L0_attn_kn_w': _L0_attn_in['kn_w'], 'L0_attn_Wg': _L0_attn_in['Wg'], 'L0_attn_head_decay': _L0_attn_in['head_decay'], 'L0_attn_temperature': _L0_attn_in['temperature'], 'L0_attn_Wp': _L0_attn_in['Wp'], 'L0_attn_mem_w': _L0_attn_in['mem_w'], 'L0_ffn_Wr': _L0_ffn_in['Wr'], 'L0_ffn_br': _L0_ffn_in['br'], 'L0_ffn_W1': _L0_ffn_in['W1'], 'L0_ffn_b1': _L0_ffn_in['b1'], 'L0_ffn_W2': _L0_ffn_in['W2'], 'L0_ffn_b2': _L0_ffn_in['b2'], 'L1_attn_video_embeds': _L1_attn_in['video_embeds'], 'L1_attn_Wq': _L1_attn_in['Wq'], 'L1_attn_bq': _L1_attn_in['bq'], 'L1_attn_Wk': _L1_attn_in['Wk'], 'L1_attn_bk': _L1_attn_in['bk'], 'L1_attn_Wv': _L1_attn_in['Wv'], 'L1_attn_bv': _L1_attn_in['bv'], 'L1_attn_Wo': _L1_attn_in['Wo'], 'L1_attn_bo': _L1_attn_in['bo'], 'L1_ffn_router_w': _L1_ffn_in['router_w'], 'L1_ffn_w1': _L1_ffn_in['w1'], 'L1_ffn_b1': _L1_ffn_in['b1'], 'L1_ffn_w2': _L1_ffn_in['w2'], 'L1_ffn_b2': _L1_ffn_in['b2'], 'L1_ffn_gamma': _L1_ffn_in['gamma'], 'L1_ffn_beta': _L1_ffn_in['beta']}

def reference(x, L0_tok_W, L0_tok_b, L0_attn_ln_w, L0_attn_Wc, L0_attn_Wqkv, L0_attn_Wreso, L0_attn_qn_w, L0_attn_kn_w, L0_attn_Wg, L0_attn_head_decay, L0_attn_temperature, L0_attn_Wp, L0_attn_mem_w, L0_ffn_Wr, L0_ffn_br, L0_ffn_W1, L0_ffn_b1, L0_ffn_W2, L0_ffn_b2, L1_attn_video_embeds, L1_attn_Wq, L1_attn_bq, L1_attn_Wk, L1_attn_bk, L1_attn_Wv, L1_attn_bv, L1_attn_Wo, L1_attn_bo, L1_ffn_router_w, L1_ffn_w1, L1_ffn_b1, L1_ffn_w2, L1_ffn_b2, L1_ffn_gamma, L1_ffn_beta):
    import jax
    import jax.numpy as jnp

    def _L0_tok_ref(x, W, b):
        import jax, jax.numpy as jnp
        import numpy as np
        BLOCK = 128
        TOP_K = 16
        B, S, D = x.shape
        n_blocks = S // BLOCK
        scores = jnp.einsum('bsd,d->bs', x, W[0]) + b[0]
        block_scores = scores.reshape(B, n_blocks, BLOCK)
        _, top_idx = jax.lax.top_k(block_scores, TOP_K)
        offsets = (jnp.arange(n_blocks, dtype=top_idx.dtype) * BLOCK)[None, :, None]
        sel_idx = (top_idx + offsets).reshape(B, n_blocks * TOP_K)
        selected_tokens = jnp.take_along_axis(x, sel_idx[:, :, None], axis=1)
        return selected_tokens

    def _L0_attn_ref(x, ln_w, Wc, Wqkv, Wreso, qn_w, kn_w, Wg, head_decay, temperature, Wp, mem_w):
        import jax, jax.numpy as jnp
        import numpy as np
        import math
        N_HEADS = 4
        EPS = 1e-06

        def rmsnorm(x, w, eps=EPS):
            xf = x.astype(jnp.float32)
            rms = jax.lax.rsqrt(jnp.mean(xf * xf, axis=-1, keepdims=True) + eps)
            return w * (xf * rms)

        def rope(x):
            L, d = (x.shape[1], x.shape[-1])
            inv_freq = 1.0 / 10000.0 ** (jnp.arange(0, d, 2, dtype=jnp.float32) / d)
            t = jnp.arange(L, dtype=jnp.float32)
            freqs = jnp.outer(t, inv_freq)
            emb = jnp.concatenate([freqs, freqs], axis=-1)
            cos = jnp.cos(emb)[None, :, None, :]
            sin = jnp.sin(emb)[None, :, None, :]
            x1, x2 = jnp.split(x, 2, axis=-1)
            x_rot = jnp.concatenate([-x2, x1], axis=-1)
            return x * cos + x_rot * sin
        B, L, D = x.shape
        H = N_HEADS
        dh = D // H
        x_norm = rmsnorm(x, ln_w)
        latent = jax.nn.silu(x_norm @ Wc)
        q, k, v = jnp.split(latent @ Wqkv, 3, axis=-1)
        q = q.reshape(B, L, H, dh)
        k = k.reshape(B, L, H, dh)
        v = v.reshape(B, L, H, dh)
        q = rope(rmsnorm(q, qn_w))
        k = rope(rmsnorm(k, kn_w))
        q_f = jax.nn.elu(q.astype(jnp.float32)) + 1.0
        k_f = jax.nn.elu(k.astype(jnp.float32)) + 1.0
        v_f = v.astype(jnp.float32)
        params = (latent @ Wreso).reshape(B, L, H, 4)
        sem_amp = jax.nn.sigmoid(params[..., 0])
        sem_phase = jax.nn.sigmoid(params[..., 1]) * math.pi
        ctx_amp = jax.nn.sigmoid(params[..., 2])
        ctx_phase = jax.nn.sigmoid(params[..., 3]) * math.pi
        raw_decay = 0.3 + 0.65 * jax.nn.sigmoid(head_decay)
        decay_rate = jnp.clip(raw_decay, 1e-05, 0.999)
        dt = 1.0 - decay_rate
        cos_diff = jnp.cos(sem_phase - ctx_phase)
        base_gate = jax.nn.sigmoid(sem_amp * ctx_amp * cos_diff * temperature)
        gate = jnp.clip(base_gate * 1.2 - 0.1, 0.05, 0.95)
        kv_input = jnp.einsum('blhd,blhe->blhde', k_f, v_f) * gate[..., None, None] * dt[None, None, :, None, None]
        z_input = k_f * dt[None, None, :, None]
        log_decay = jnp.log(decay_rate)
        cld = jnp.arange(1, L + 1, dtype=jnp.float32)[None, :, None] * log_decay[None, None, :]
        df = jnp.exp(cld)[..., None]
        safe_z = df + 1e-08
        kv_states = jnp.cumsum(kv_input / safe_z[..., None], axis=1) * df[..., None]
        z_states = jnp.cumsum(z_input / safe_z, axis=1) * df
        out_num = jnp.einsum('blhd,blhde->blhe', q_f, kv_states)
        den = jnp.clip(jnp.sum(q_f * z_states, axis=-1, keepdims=True), 1e-05, None)
        out = rmsnorm((out_num / den).reshape(B, L, D), mem_w)
        gate_val = jax.nn.silu(latent @ Wg)
        return out @ Wp * gate_val

    def _L0_ffn_ref(x, Wr, br, W1, b1, W2, b2):
        import jax, jax.numpy as jnp
        import numpy as np
        B, S, D = (8, 1024, 128)
        H = 512
        O = 128
        E = 8
        TOP_K = 1
        b, s, d = x.shape
        xf = x.reshape(-1, d)
        router_logits = xf @ Wr + br
        topk_logits, topk_idx = jax.lax.top_k(router_logits, TOP_K)
        topk_gates = jax.nn.softmax(topk_logits, axis=1)
        out = jnp.zeros((xf.shape[0], O), dtype=x.dtype)
        for k in range(TOP_K):
            idx_k = topk_idx[:, k]
            gate_k = topk_gates[:, k:k + 1]
            for e in range(E):
                h = jax.nn.relu(xf @ W1[e] + b1[e])
                oe = h @ W2[e] + b2[e]
                mask = (idx_k == e)[:, None]
                out = out + jnp.where(mask, gate_k * oe, 0.0)
        return out.reshape(b, s, O)

    def _L1_attn_ref(text_embeds, video_embeds, Wq, bq, Wk, bk, Wv, bv, Wo, bo):
        import math
        import jax, jax.numpy as jnp
        import numpy as np
        EMBED = 128
        HEADS = 2
        HEAD_DIM = EMBED // HEADS
        num_texts, num_words, _ = text_embeds.shape
        num_vids, num_frames, _ = video_embeds.shape
        q = (text_embeds @ Wq.T + bq).reshape(num_texts, num_words, HEADS, HEAD_DIM)
        k = (video_embeds @ Wk.T + bk).reshape(num_vids, num_frames, HEADS, HEAD_DIM)
        v = (video_embeds @ Wv.T + bv).reshape(num_vids, num_frames, HEADS, HEAD_DIM)
        logits = jnp.einsum('avhd,bthd->abhvt', k, q) / math.sqrt(HEAD_DIM)
        weights = jax.nn.softmax(logits, axis=3)
        attn = jnp.einsum('avhd,abhvt->abhtd', v, weights)
        attn = attn.reshape(num_vids, num_texts, num_words, EMBED)
        attn = attn.mean(axis=0)
        return attn @ Wo.T + bo

    def _L1_ffn_ref(x, router_w, w1, b1, w2, b2, gamma, beta):
        import jax, jax.numpy as jnp
        import numpy as np
        K = 2
        EPS = 1e-06

        def _layernorm(x, gamma, beta):
            mu = jnp.mean(x, axis=-1, keepdims=True)
            var = jnp.mean(jnp.square(x - mu), axis=-1, keepdims=True)
            return (x - mu) * jax.lax.rsqrt(var + EPS) * gamma + beta
        B, S, D = x.shape
        E = w1.shape[0]
        xf = x.reshape(-1, D)
        logits = xf @ router_w
        gate_vals, idx = jax.lax.top_k(logits, K)
        gates = jax.nn.softmax(gate_vals, axis=-1)
        out = jnp.zeros_like(xf)
        for e in range(E):
            h = jax.nn.relu(xf @ w1[e] + b1[e]) @ w2[e] + b2[e]
            y = _layernorm(xf + h, gamma[e], beta[e])
            w = jnp.sum(jnp.where(idx == e, gates, 0.0), axis=-1)
            out = out + w[:, None] * y
        return out.reshape(B, S, D)
    h = _L0_tok_ref(x, L0_tok_W, L0_tok_b)
    h = h + _L0_attn_ref(_layernorm(h, axis=-1), L0_attn_ln_w, L0_attn_Wc, L0_attn_Wqkv, L0_attn_Wreso, L0_attn_qn_w, L0_attn_kn_w, L0_attn_Wg, L0_attn_head_decay, L0_attn_temperature, L0_attn_Wp, L0_attn_mem_w)
    h = h + _L0_ffn_ref(_layernorm(h, axis=-1), L0_ffn_Wr, L0_ffn_br, L0_ffn_W1, L0_ffn_b1, L0_ffn_W2, L0_ffn_b2)
    h = h + _L1_attn_ref(_layernorm(h, axis=-1), L1_attn_video_embeds, L1_attn_Wq, L1_attn_bq, L1_attn_Wk, L1_attn_bk, L1_attn_Wv, L1_attn_bv, L1_attn_Wo, L1_attn_bo)
    h = h + _L1_ffn_ref(_layernorm(h, axis=-1), L1_ffn_router_w, L1_ffn_w1, L1_ffn_b1, L1_ffn_w2, L1_ffn_b2, L1_ffn_gamma, L1_ffn_beta)
    return h

_drawn_inputs = setup_inputs


def setup_inputs(seed=0):
    import zlib

    import numpy as np

    out = dict(_drawn_inputs(seed))
    spreads = {'L0_attn_ln_w': (1.0, 0.6),
     'L0_attn_qn_w': (1.0, 0.6),
     'L0_attn_kn_w': (1.0, 0.6),
     'L0_attn_mem_w': (1.0, 0.6),
     'L0_ffn_br': (0.0, 0.272),
     'L0_ffn_b1': (0.0, 0.8),
     'L0_ffn_b2': (0.0, 0.33),
     'L1_attn_bq': (0.0, 0.646),
     'L1_attn_bk': (0.0, 2.0),
     'L1_attn_bv': (0.0, 0.307),
     'L1_attn_bo': (0.0, 0.336),
     'L1_ffn_b1': (0.0, 0.718),
     'L1_ffn_b2': (0.0, 0.592),
     'L1_ffn_gamma': (1.0, 0.579),
     'L1_ffn_beta': (0.0, 0.604)}
    factors = {'L0_attn_Wc': 8.0,
     'L0_attn_Wqkv': 8.0,
     'L0_attn_Wreso': 8.0,
     'L0_attn_Wg': 8.0,
     'L0_attn_head_decay': 8.0,
     'L0_attn_Wp': 8.0,
     'L1_attn_video_embeds': 2.806,
     'L0_ffn_W1': 3.565,
     'L0_ffn_W2': 2.836,
     'L1_ffn_w1': 5.94}
    for name, (base, spread) in spreads.items():
        noise = np.random.default_rng([zlib.crc32(name.encode()), seed]).standard_normal(out[name].shape)
        drawn = base * np.exp(spread * noise) if base else spread * noise
        out[name] = jnp.asarray(drawn.astype(out[name].dtype))
    for name, factor in factors.items():
        out[name] = (out[name] * factor).astype(out[name].dtype)
    return out
```

```python
from contextlib import ExitStack

import numpy as np

import concourse.bass as bass
from concourse import mybir

F32 = mybir.dt.float32
F32R = mybir.dt.float32r
BF16 = mybir.dt.bfloat16
I32 = mybir.dt.int32
U32 = mybir.dt.uint32
ALU = mybir.AluOpType
ACT = mybir.ActivationFunctionType
X = mybir.AxisListType.X
ds = bass.ds

P = 128
B, S, D = 8, 4096, 128
BLOCK, TOP = 128, 16
L = S // BLOCK * TOP
N = B * L
G = N // P
TB = L // P
LAT, H0, DH0 = 64, 4, 32
V1 = DH0 + 1
QKV = 3 * D + 4 * H0
E, F = 8, 512
FC = F // P
VID, FR, H1, DH1 = 128, 64, 2, 64
KEYS = VID * FR
KC = 512
VC = KC // FR
NKC = KEYS // KC
SUB = KC // P
SLOT_TILES = {1: G + E, 2: 2 * G + E}
LN_EPS, RMS_EPS = 1e-5, 1e-6
BIG = 1e30


def shape_constants():
    p = np.arange(P)
    block = np.zeros((P, H0, V1))
    for h in range(H0):
        block[h * DH0:(h + 1) * DH0, h] = 1.0
    pos = np.arange(TB)[None, :] * P + p[:, None]
    inv = (1.0 / np.float32(10000.0) ** (np.arange(0, DH0, 2, dtype=np.float32) / DH0)).astype(np.float32)
    ang = pos[..., None].astype(np.float32) * inv
    e = np.arange(E)

    def row(v):
        return np.broadcast_to(np.asarray(v, np.float64).reshape(1, -1), (P, np.size(v)))

    cols = {
        "ident": np.eye(P),
        "causal": (p[None, :] >= p[:, None]) * 1.0,
        "before": (p[:, None] < p[None, :]) * 1.0,
        "headblock": block.reshape(P, -1),
        "cos": np.concatenate([np.cos(ang), np.cos(ang)], -1).reshape(P, -1),
        "sin": np.concatenate([-np.sin(ang), np.sin(ang)], -1).reshape(P, -1),
        "steps": pos + 1.0,
        "blockrow": np.stack([p * BLOCK, (p + P) * BLOCK], 1),
        "descend": row(E - e),
        "tiles128": row(np.arange(G) * P),
        "earlier": row((e[None, :] < e[:, None]) * 1.0),
        "minus_half": np.full((P, 1), -0.5),
        "slot": row(np.arange(SLOT_TILES[2])),
    }
    at, off = {}, 0
    for k, v in cols.items():
        at[k] = slice(off, off + v.shape[1])
        off += v.shape[1]
    return at, np.concatenate(list(cols.values()), 1).astype(np.float32)


AT, CONSTANTS = shape_constants()


class Steps:

    def __init__(self, engine, semaphore):
        self.engine, self.semaphore, self.base, self.k = engine, semaphore, 0, 0

    def mark(self, instruction):
        instruction.then_inc(self.semaphore, 1)
        self.k += 1

    def wait(self):
        self.engine.wait_ge(self.semaphore, self.base + self.k)

    def wait_apart(self, mark):
        self.wait()
        self.engine.memset(mark, 0.0)

    def then(self, instruction):
        self.mark(instruction)
        self.wait()

    def turn(self, i, per):
        self.outer, self.per = self.base + self.k, per
        self.base, self.k = self.outer + i * per, 0

    def end(self, turns):
        assert self.k == self.per, (self.k, self.per)
        self.base, self.k = self.outer + turns * self.per, 0


class Kept:

    def __init__(self, nc, ctx, has):
        def sb(n, s, d=F32):
            return ctx.enter_context(nc.sbuf_tensor(n, s, d))

        self.consts = sb("consts", [P, CONSTANTS.shape[1]])
        self.hidden = sb("hidden", [P, G, D])
        self.keys = sb("keys", [P, H1 * KEYS], F32R)
        self.values = sb("values", [P, H1, KEYS // P, DH1])
        self.wq2 = sb("wq2", [P, H1, P])
        self.wo2 = sb("wo2", [P, 2, D])
        self.bq2 = sb("bq2", [P, H1])
        self.bo_all = sb("bo_all", [P, D])
        self.neg_ident = sb("neg_ident", [P, P], F32R)
        self.rows_dram = nc.dram_tensor("chosen_rows", [N], U32).ap()
        self.routed_dram = {k: nc.dram_tensor(f"routed{k}", [t * P, D], F32).ap() for k, t in SLOT_TILES.items()}
        self.result_dram = {k: nc.dram_tensor(f"result{k}", [t * P, D], F32).ap() for k, t in SLOT_TILES.items()}

    def const(self, name):
        return self.consts[:, AT[name]]


def inverse_root(pool, K, out, square):
    return pool.tensor_tensor(out, square, K.const("minus_half").to_broadcast([P, square.shape[1]]), ALU.pow)


def column(vector):
    return vector.rearrange("(p a) -> p a", a=1)


def everywhere(vector, width):
    return vector.rearrange("(a n) -> a n", a=1).to_broadcast([P, width])


def allocators(nc, ctx, phase):
    return (lambda n, s, d=F32: ctx.enter_context(nc.sbuf_tensor(f"{phase}_{n}", s, d)),
            lambda n, s, d=F32: ctx.enter_context(nc.psum_tensor(f"{phase}_{n}", s, d)),
            lambda n: ctx.enter_context(nc.semaphore(f"{phase}_{n}")))


def clear_semaphores(nc, first, last):
    with nc.Block() as block:
        @block.gpsimd
        def _(pool):
            pool.sem_clear(range(first.num, last.num + 1))


class LayerNorm:

    def __init__(self, nc, ctx, phase):
        sb, _, sem = allocators(nc, ctx, phase)
        self.rows = sb("rows", [P, TB, D])
        self.stats, self.mv = sb("stats", [P, TB, 6]), sb("mv", [P, TB, 2])
        self.square, self.root = sb("square", [P, TB]), sb("root", [P, TB])
        self.steps, self.square_ready, self.root_ready = sem("norm_steps"), sem("square_ready"), sem("root_ready")
        self.pause = sb("pause", [P, 1])
        self.marks = 2 * TB

    def on_vector(self, dve, steps, b, hidden, used, ready):
        for i in range(TB):
            steps.mark(dve.bn_stats(self.stats[:, i, :], hidden[:, ds(b * TB + i, 1), :].rearrange("p a d -> p (a d)")))
        steps.wait_apart(self.pause[:])
        for i in range(TB):
            steps.mark(dve.bn_aggr(self.mv[:, i, :], self.stats[:, i, :]))
        steps.wait()
        dve.tensor_scalar(self.square[:], self.mv[:, :, 1], LN_EPS, None, ALU.add).then_inc(self.square_ready, 1)
        dve.wait_ge(self.root_ready, b + 1)
        dve.wait_ge(used, b)
        for i in range(TB):
            ins = dve.tensor_scalar(self.rows[:, i, :], hidden[:, ds(b * TB + i, 1), :].rearrange("p a d -> p (a d)"),
                                    self.mv[:, i, 0:1], self.root[:, i:i + 1], ALU.subtract, ALU.mult)
        ins.then_inc(ready, 1)

    def on_pool(self, pool, K, b, ready):
        pool.wait_ge(self.square_ready, b + 1)
        pool.wait_ge(ready, b)
        inverse_root(pool, K, self.root[:], self.square[:]).then_inc(self.root_ready, 1)


def select_and_project(nc, a, K):
    with ExitStack() as ctx:
        sb, ps, sem = allocators(nc, ctx, "select")
        CT = 8
        TURNS = BLOCK // CT // 4
        xbuf = sb("xbuf", [P, 4, 2, CT, D])
        prod = sb("prod", [P, 2, 2, CT, D])
        wtok = sb("wtok", [P, D])
        btok = sb("btok", [P, 1])
        scores = sb("scores", [P, 2, BLOCK])
        rest = sb("rest", [P, 2, BLOCK])
        best = sb("best", [P, 2, TOP])
        besti = sb("besti", [P, 2, TOP], U32)
        rows = sb("rows", [P, 2, TOP], U32)
        rowidx = sb("rowidx", [P, G], U32)
        wraw = sb("wraw", [P, 5, D])
        wk2 = sb("wk2", [P, H1, P])
        wvT = sb("wvT", [P, D])
        bk2 = sb("bk2", [P, H1])
        bv_all = sb("bv_all", [P, D])
        emb = sb("emb", [P, 4, SUB, D])
        embT = sb("embT", [P, 2, KC])
        psT = ps("psT", [P, 2, KC])
        psK = ps("psK", [P, H1, KC])
        psV = ps("psV", [P, 2, KC])
        gathered, consts_in, weights_in = sem("gathered"), sem("consts_in"), sem("weights_in")
        x_in = [sem(f"x_in{i}") for i in range(4)]
        emb_in = [sem(f"emb_in{i}") for i in range(4)]
        odd_products, chunks_reduced, select_steps = sem("odd_products"), sem("chunks_reduced"), sem("select_steps")
        weightT_ready, weightT_copied = sem("weightT_ready"), sem("weightT_copied")
        embT_ready, embT_copied = sem("embT_ready"), sem("embT_copied")
        keys_ready, values_ready = sem("keys_ready"), sem("values_ready")
        key_highs, key_lows, values_done = sem("key_highs"), sem("key_lows"), sem("values_done")
        rows_chosen, rows_out, rows_back = sem("rows_chosen"), sem("rows_out"), sem("rows_back")

        weights_landed = 16 * (7 + 4 * H1 + 2)

        x_chunks = a["x"].rearrange("b (k t) d -> (b k) (t d)", t=BLOCK).rearrange("(f p) n -> p f n", p=P)
        emb_rows = a["L1_attn_video_embeds"].rearrange("v f d -> (v f) d").rearrange("(t p) d -> p t d", p=P)
        ident = K.const("ident")
        per_token = [P, 2 * CT, D]

        with nc.Block() as block:
            @block.sync
            def _(sp):
                sp.dma_start(K.consts[:], a["shape_constants"]).then_inc(consts_in, 16)
                sp.dma_start(wtok[:], everywhere(a["L0_tok_W"].rearrange("a n -> (a n)"), D)).then_inc(consts_in, 16)
                sp.dma_start(btok[:], everywhere(a["L0_tok_b"], 1)).then_inc(consts_in, 16)

                def load(c, s):
                    sp.dma_start(xbuf[:, s, :, :, :].rearrange("p f t d -> p f (t d)"),
                                 x_chunks[:, :, ds(c * CT * D, CT * D)]).then_inc(x_in[s], 16)

                for s in range(4):
                    load(s, s)
                with sp.Fori(1, TURNS) as it:
                    for s in range(4):
                        sp.wait_ge(chunks_reduced, (it - 1) * 4 + s + 1)
                        load(it * 4 + s, s)
                sp.wait_ge(rows_chosen, 2)
                sp.dma_start(K.rows_dram.rearrange("(f p r) -> p f r", p=P, r=TOP), rows[:]).then_inc(rows_out, 16)
                sp.wait_ge(rows_out, 16)
                sp.dma_start(rowidx[:], K.rows_dram.rearrange("(g p) -> p g", p=P),
                             allow_slow_non_contiguous=True).then_inc(rows_back, 16)

            @block.gpsimd
            def _(pool):
                pool.wait_ge(consts_in, 48)
                with pool.Fori(0, TURNS) as it:
                    for s in (1, 3):
                        pool.wait_ge(x_in[s], (it + 1) * 16)
                        pool.wait_ge(chunks_reduced, it * 4 + s - 1)
                        pool.tensor_tensor(prod[:, 1].rearrange("p f t d -> p (f t) d"),
                                           xbuf[:, s].rearrange("p f t d -> p (f t) d"),
                                           wtok[:, None, :].to_broadcast(per_token), ALU.mult).then_inc(odd_products, 1)
                pool.wait_ge(rows_back, 16)
                for g in range(G):
                    pool.indirect_dma_start(K.hidden[:, g, :], None, a["x"].rearrange("b s d -> (b s) d"),
                                            bass.IndirectOffsetOnAxis(ap=rowidx[:, g:g + 1], axis=0)).then_inc(gathered, 16)
                pool.wait_ge(gathered, 16 * G)

            @block.vector
            def _(dve):
                steps = Steps(dve, select_steps)
                dve.wait_ge(consts_in, 48)
                steps.mark(dve.tensor_scalar(K.neg_ident[:], ident, -1.0, None, ALU.mult))
                dve.wait_ge(weights_in, weights_landed)
                with dve.Fori(0, TURNS) as it:
                    steps.turn(it, 2)
                    for s in range(4):
                        c = it * 4 + s
                        if s % 2 == 0:
                            dve.wait_ge(x_in[s], (it + 1) * 16)
                            steps.then(dve.tensor_tensor(prod[:, 0].rearrange("p f t d -> p (f t) d"),
                                                         xbuf[:, s].rearrange("p f t d -> p (f t) d"),
                                                         wtok[:, None, :].to_broadcast(per_token), ALU.mult))
                        else:
                            dve.wait_ge(odd_products, it * 2 + s // 2 + 1)
                        dve.tensor_reduce(scores[:, :, ds(c * CT, CT)], prod[:, s % 2], X, ALU.add).then_inc(chunks_reduced, 1)
                        if s % 2 == 0:
                            dve.wait_ge(chunks_reduced, c + 1)
                        for h in range(H1):
                            dve.wait_ge(key_highs, c * H1 + h + 1)
                            cols = ds(c * KC + h * KEYS, KC)
                            dve.scalar_tensor_tensor(K.keys[64:P, cols], psK[64:P, h, :], bk2[64:P, h:h + 1],
                                                     K.keys[64:P, cols].bitcast(F32), ALU.add, ALU.subtract).then_inc(key_lows, 1)
                        dve.wait_ge(values_ready, c + 1)
                        dve.tensor_tensor(K.values[:, :, ds(c * SUB, SUB), :].rearrange("p h t e -> p t h e"),
                                          psV[:, s % 2, :].rearrange("p (t h e) -> p t h e", t=SUB, h=H1),
                                          bv_all[:].rearrange("p (h e) -> p h e", h=H1)[:, None].to_broadcast([P, SUB, H1, DH1]),
                                          ALU.add).then_inc(values_done, 1)
                steps.end(TURNS)
                dve.wait_ge(chunks_reduced, 4 * TURNS)
                steps.then(dve.tensor_scalar(scores[:], scores[:], btok[:, 0:1], None, ALU.add))
                for f in range(2):
                    steps.then(dve.max(best[:, f, 0:8], scores[:, f, :]))
                    steps.mark(dve.max_index(besti[:, f, 0:8], best[:, f, 0:8], scores[:, f, :]))
                    steps.then(dve.match_replace(rest[:, f, :], best[:, f, 0:8], scores[:, f, :], -3e38))
                    steps.then(dve.max(best[:, f, 8:16], rest[:, f, :]))
                    steps.then(dve.max_index(besti[:, f, 8:16], best[:, f, 8:16], rest[:, f, :]))
                    dve.tensor_scalar(rows[:, f, :], besti[:, f, :], K.const("blockrow")[:, f:f + 1], None,
                                      ALU.add).then_inc(rows_chosen, 1)

            @block.scalar
            def _(act):
                for j, n in enumerate(("Wq", "Wk", "Wv")):
                    act.dma_start(wraw[:, j, :], a["L1_attn_" + n]).then_inc(weights_in, 16)
                for side in range(2):
                    for copy in range(2):
                        act.dma_start(wraw[:, 3 + side, copy * DH1:(copy + 1) * DH1],
                                      a["L1_attn_Wo"][:, side * DH1:(side + 1) * DH1]).then_inc(weights_in, 16)
                for h in range(H1):
                    for part in (slice(0, 64), slice(64, P)):
                        act.dma_start(bk2[part, h:h + 1], column(a["L1_attn_bk"][h * DH1:(h + 1) * DH1])).then_inc(weights_in, 16)
                        act.dma_start(K.bq2[part, h:h + 1], column(a["L1_attn_bq"][h * DH1:(h + 1) * DH1])).then_inc(weights_in, 16)
                act.dma_start(bv_all[:], everywhere(a["L1_attn_bv"], D)).then_inc(weights_in, 16)
                act.dma_start(K.bo_all[:], everywhere(a["L1_attn_bo"], D)).then_inc(weights_in, 16)

                def load(c, s):
                    act.dma_start(emb[:, s], emb_rows[:, ds(c * SUB, SUB), :]).then_inc(emb_in[s], 16)

                for s in range(4):
                    load(s, s)
                act.wait_ge(weightT_ready, 5)
                for h in range(H1):
                    for part in range(2):
                        half = slice(part * DH1, (part + 1) * DH1)
                        head = slice(h * DH1, (h + 1) * DH1)
                        act.activation(K.wq2[:, h, half], psT[:, 0, 0:D][:, head], ACT.Copy).then_inc(weightT_copied, 1)
                        act.activation(wk2[:, h, half], psT[:, 0, D:2 * D][:, head], ACT.Copy).then_inc(weightT_copied, 1)
                act.activation(wvT[:], psT[:, 0, 2 * D:3 * D], ACT.Copy).then_inc(weightT_copied, 1)
                for side in range(2):
                    act.activation(K.wo2[:, side, :], psT[:, side, 3 * D:4 * D], ACT.Copy).then_inc(weightT_copied, 1)

                def chunk(c, s, ahead):
                    act.wait_ge(embT_ready, c + 1)
                    act.activation(embT[:, s % 2, :], psT[:, s % 2, :], ACT.Copy).then_inc(embT_copied, 1)
                    if ahead:
                        load(c + 4, s)
                    for h in range(H1):
                        act.wait_ge(keys_ready, c * H1 + h + 1)
                        act.activation(K.keys[:, ds(c * KC + h * KEYS, KC)], psK[:, h, :], ACT.Identity,
                                       bias=bk2[:, h:h + 1]).then_inc(key_highs, 1)

                with act.Fori(0, TURNS - 1) as it:
                    for s in range(4):
                        chunk(it * 4 + s, s, True)
                for s in range(4):
                    chunk((TURNS - 1) * 4 + s, s, False)

            @block.tensor
            def _(pe):
                pe.wait_ge(consts_in, 48)
                pe.wait_ge(weights_in, weights_landed)
                for j in range(5):
                    at = min(j, 3) * D
                    pe.transpose(psT[:, j // 4, at:at + D], wraw[:, j, :], ident).then_inc(weightT_ready, 1)
                pe.wait_ge(weightT_copied, 4 * H1 + 3)
                with pe.Fori(0, TURNS) as it:
                    for s in range(4):
                        c = it * 4 + s
                        pe.wait_ge(emb_in[s], (it + 1) * 16)
                        for t in range(SUB):
                            mm = pe.transpose(psT[:, s % 2, t * P:(t + 1) * P], emb[:, s, t, :], ident)
                        mm.then_inc(embT_ready, 1)
                        pe.wait_ge(embT_copied, c + 1)
                        pe.wait_ge(key_lows, c * H1)
                        for h in range(H1):
                            pe.matmul(psK[:, h, :], wk2[:, h, :], embT[:, s % 2, :], start=True, stop=True).then_inc(keys_ready, 1)
                        if s < 2:
                            pe.wait_ge(values_done, it * 4)
                        else:
                            pe.wait_ge(values_done, c - 1)
                        for t in range(SUB):
                            mm = pe.matmul(psV[:, s % 2, t * P:(t + 1) * P], embT[:, s % 2, t * P:(t + 1) * P], wvT[:],
                                           start=True, stop=True, skip_group_check=True)
                        mm.then_inc(values_ready, 1)

        clear_semaphores(nc, consts_in, rows_back)


def zero_dram(sp, K, zeros, done):
    for k, tiles in SLOT_TILES.items():
        view = K.routed_dram[k].rearrange("(n p) d -> p n d", p=P)
        for j in range(0, tiles, E):
            sp.dma_start(view[:, j:j + E, :], zeros[:]).then_inc(done, 16)


def retention(nc, a, K):
    with ExitStack() as ctx:
        sb, _, sem = allocators(nc, ctx, "retention")
        qkv = sb("qkv", [P, G, 3 * D])
        gate_out = sb("gate_out", [P, G, D])
        params = sb("params", [P, G, H0, 4])
        gate = sb("gate", [P, G, H0])
        decay = sb("decay", [P, TB, H0])
        kscale = sb("kscale", [P, TB, H0])
        rope_c = sb("rope_c", [P, TB, 2, DH0])
        rope_s = sb("rope_s", [P, TB, 2, DH0])
        wp = sb("wp", [P, D])
        s_const, s_a, s_latent, s_gates = sem("ret_weights_in"), sem("xn_steps"), sem("latent_ready"), sem("gate_steps")
        xn_ready, xnT_ready, xnT_copied = sem("xn_ready"), sem("xnT_ready"), sem("xnT_copied")
        latent_done, qkv_ready, qkv_copied = sem("latent_done"), sem("qkv_ready"), sem("qkv_copied")
        gate_ready, gate_done = sem("gate_ready"), sem("gate_done")
        ident = K.const("ident")

        with ExitStack() as inner:
            sb1, ps1, _ = allocators(nc, inner, "project")
            zeros = sb1("zeros", [P, E, D])
            wc = sb1("wc", [P, LAT])
            wall = sb1("wall", [LAT, QKV + D])
            lnw, memw = sb1("lnw", [P, 1]), sb1("memw", [P, 1])
            qkw = sb1("qkw", [P, 2, DH0])
            temp, hd = sb1("temp", [P, 1]), sb1("hd", [P, H0])
            stats = sb1("stats", [P, TB, 6])
            mv, pause = sb1("mv", [P, TB, 2]), sb1("pause", [P, 1])
            sc = sb1("sc", [P, 4, TB])
            xn = sb1("xn", [P, TB, D])
            xnT = sb1("xnT", [P, L])
            latT = sb1("latT", [LAT, L])
            sg = sb1("sg", [P, G, H0, 4])
            dph, amp = sb1("dph", [P, G, H0]), sb1("amp", [P, G, H0])
            rate = sb1("rate", [P, 4, H0])
            cld = sb1("cld", [P, TB, H0])
            half_pi = sb1("half_pi", [P, 1])
            psT = ps1("psT", [P, L])
            psL = ps1("psL", [LAT, L])
            psQ = ps1("psQ", [P, 2, 512])
            psG = ps1("psG", [P, TB, D])
            zeroed, zeros_set = sem("routed_zeroed"), sem("zeros_set")
            square_ready, root_ready = sem("xn_square_ready"), sem("xn_root_ready")
            weights_ready, act_gates = sem("ret_weights_ready"), sem("act_gates")
            NW = 10

            with nc.Block() as block:
                @block.sync
                def _(sp):
                    sp.dma_start(wc[:], a["L0_attn_Wc"]).then_inc(s_const, 16)
                    sp.dma_start(wall[:, 0:3 * D], a["L0_attn_Wqkv"]).then_inc(s_const, 16)
                    sp.dma_start(wall[:, 3 * D:QKV], a["L0_attn_Wreso"]).then_inc(s_const, 16)
                    sp.dma_start(wall[:, QKV:QKV + D], a["L0_attn_Wg"]).then_inc(s_const, 16)
                    sp.dma_start(wp[:], a["L0_attn_Wp"]).then_inc(s_const, 16)
                    sp.dma_start(lnw[:], column(a["L0_attn_ln_w"])).then_inc(s_const, 16)
                    sp.dma_start(memw[:], column(a["L0_attn_mem_w"])).then_inc(s_const, 16)
                    sp.dma_start(qkw[:, 0, :], everywhere(a["L0_attn_qn_w"], DH0)).then_inc(s_const, 16)
                    sp.dma_start(qkw[:, 1, :], everywhere(a["L0_attn_kn_w"], DH0)).then_inc(s_const, 16)
                    sp.dma_start(temp[:], everywhere(a["L0_attn_temperature"], 1)).then_inc(s_const, 16)
                    sp.dma_start(hd[:], everywhere(a["L0_attn_head_decay"], H0)).then_inc(s_const, 16)
                    sp.wait_ge(zeros_set, 1)
                    zero_dram(sp, K, zeros, zeroed)
                    sp.wait_ge(zeroed, 16 * sum(SLOT_TILES.values()) // E)

                @block.gpsimd
                def _(pool):
                    pool.memset(zeros[:], 0.0).then_inc(zeros_set, 1)
                    with pool.Fori(0, B) as b:
                        pool.wait_ge(square_ready, b + 1)
                        pool.wait_ge(xn_ready, b)
                        inverse_root(pool, K, sc[:, 1, :], sc[:, 0, :]).then_inc(root_ready, 1)

                @block.vector
                def _(dve):
                    steps = Steps(dve, s_a)
                    dve.wait_ge(s_const, 16 * 11)
                    dve.tensor_scalar(wc[:], wc[:], lnw[:, 0:1], None, ALU.mult).then_inc(weights_ready, 1)
                    dve.tensor_scalar(wp[:], wp[:], memw[:, 0:1], None, ALU.mult).then_inc(weights_ready, 1)
                    with dve.Fori(0, B) as b:
                        steps.turn(b, 2 * TB)
                        for i in range(TB):
                            steps.mark(dve.bn_stats(stats[:, i, :], K.hidden[:, ds(b * TB + i, 1), :].rearrange("p a d -> p (a d)")))
                        steps.wait_apart(pause[:])
                        for i in range(TB):
                            steps.mark(dve.bn_aggr(mv[:, i, :], stats[:, i, :]))
                        steps.wait()
                        dve.tensor_scalar(sc[:, 0, :], mv[:, :, 1], 1.0 + RMS_EPS, LN_EPS * RMS_EPS, ALU.mult, ALU.add).then_inc(square_ready, 1)
                        dve.wait_ge(root_ready, b + 1)
                        dve.wait_ge(xnT_ready, b)
                        for i in range(TB):
                            ins = dve.tensor_scalar(xn[:, i, :], K.hidden[:, ds(b * TB + i, 1), :].rearrange("p a d -> p (a d)"),
                                                    mv[:, i, 0:1], sc[:, 1, i:i + 1], ALU.subtract, ALU.mult)
                        ins.then_inc(xn_ready, 1)
                    steps.end(B)
                    steps = Steps(dve, s_gates)
                    for j in range(2):
                        w = qkw[:, j, :]
                        cos = K.const("cos").rearrange("p (i d) -> p i d", i=TB)
                        sin = K.const("sin").rearrange("p (i d) -> p i d", i=TB)
                        hw = DH0 // 2
                        steps.mark(dve.tensor_tensor(rope_c[:, :, j, :], cos, w[:, None, :].to_broadcast([P, TB, DH0]), ALU.mult))
                        steps.mark(dve.tensor_tensor(rope_s[:, :, j, 0:hw], sin[:, :, 0:hw], w[:, None, hw:DH0].to_broadcast([P, TB, hw]), ALU.mult))
                        steps.mark(dve.tensor_tensor(rope_s[:, :, j, hw:DH0], sin[:, :, hw:DH0], w[:, None, 0:hw].to_broadcast([P, TB, hw]), ALU.mult))
                    steps.mark(dve.memset(half_pi[:], float(np.pi / 2)))
                    dve.wait_ge(act_gates, 1)
                    steps.then(dve.tensor_tensor(dph[:], sg[:, :, :, 1], sg[:, :, :, 3], ALU.subtract))
                    steps.then(dve.scalar_tensor_tensor(dph[:], dph[:], -1.0, dph[:], ALU.mult, ALU.max))
                    steps.then(dve.tensor_tensor(amp[:], sg[:, :, :, 0], sg[:, :, :, 2], ALU.mult))
                    dve.wait_ge(act_gates, 3)
                    steps.then(dve.tensor_tensor(amp[:], amp[:], gate[:], ALU.mult))
                    steps.then(dve.tensor_scalar(amp[:], amp[:], temp[:, 0:1], None, ALU.mult))
                    steps.then(dve.tensor_scalar(rate[:, 1, :], rate[:, 0, :], 0.65, 0.3, ALU.mult, ALU.add))
                    steps.then(dve.tensor_scalar(rate[:, 2, :], rate[:, 1, :], 1e-5, 0.999, ALU.max, ALU.min))
                    steps.then(dve.tensor_scalar(rate[:, 3, :], rate[:, 2, :], -1.0, 1.0, ALU.mult, ALU.add))
                    dve.wait_ge(act_gates, 5)
                    steps.then(dve.tensor_tensor(cld[:], K.const("steps")[:, :, None].to_broadcast([P, TB, H0]),
                                                 rate[:, 0:1, :].to_broadcast([P, TB, H0]), ALU.mult))
                    steps.then(dve.tensor_scalar(gate[:], gate[:], 1.2, -0.1, ALU.mult, ALU.add))
                    steps.then(dve.tensor_scalar(gate[:], gate[:], 0.05, 0.95, ALU.max, ALU.min))
                    dve.wait_ge(act_gates, 6)
                    steps.then(dve.tensor_scalar(kscale[:], decay[:], 1e-8, None, ALU.add))
                    steps.then(dve.reciprocal(kscale[:], kscale[:]))
                    steps.then(dve.tensor_tensor(kscale[:], kscale[:], rate[:, 3:4, :].to_broadcast([P, TB, H0]), ALU.mult))

                @block.scalar
                def _(act):
                    with act.Fori(0, B) as b:
                        act.wait_ge(xnT_ready, b + 1)
                        act.activation(xnT[:], psT[:], ACT.Copy).then_inc(xnT_copied, 1)
                        act.wait_ge(s_latent, b + 1)
                        act.activation(latT[:], psL[:], ACT.Silu).then_inc(latent_done, 1)
                        for i in range(TB):
                            act.wait_ge(qkv_ready, b * TB + i + 1)
                            act.activation(qkv[:, ds(b * TB + i, 1), :].rearrange("p a d -> p (a d)"), psQ[:, i % 2, 0:3 * D], ACT.Copy)
                            act.activation(params[:, ds(b * TB + i, 1)].rearrange("p a h c -> p (a h c)"), psQ[:, i % 2, 3 * D:QKV], ACT.Copy).then_inc(qkv_copied, 1)
                        act.wait_ge(gate_ready, b + 1)
                        act.activation(gate_out[:, ds(b * TB, TB), :], psG[:], ACT.Silu).then_inc(gate_done, 1)
                    act.wait_ge(qkv_copied, G)
                    act.activation(sg[:], params[:], ACT.Sigmoid).then_inc(act_gates, 1)
                    act.activation(rate[:, 0, :], hd[:], ACT.Sigmoid).then_inc(act_gates, 1)
                    act.wait_ge(s_gates, 9)
                    act.activation(gate[:], dph[:], ACT.Sin, bias=half_pi[:, 0:1], scale=-float(np.pi)).then_inc(act_gates, 1)
                    act.wait_ge(s_gates, 12)
                    act.activation(gate[:], amp[:], ACT.Sigmoid).then_inc(act_gates, 1)
                    act.wait_ge(s_gates, 14)
                    act.activation(rate[:, 0, :], rate[:, 2, :], ACT.Ln).then_inc(act_gates, 1)
                    act.wait_ge(s_gates, 16)
                    act.activation(decay[:], cld[:], ACT.Exp).then_inc(act_gates, 1)

                @block.tensor
                def _(pe):
                    pe.wait_ge(weights_ready, 2)
                    with pe.Fori(0, B) as b:
                        pe.wait_ge(xn_ready, b + 1)
                        for i in range(TB):
                            mm = pe.transpose(psT[:, i * P:(i + 1) * P], xn[:, i, :], ident)
                        mm.then_inc(xnT_ready, 1)
                        pe.wait_ge(xnT_copied, b + 1)
                        pe.matmul(psL[:], wc[:], xnT[:], start=True, stop=True).then_inc(s_latent, 1)
                        pe.wait_ge(latent_done, b + 1)
                        pe.wait_ge(qkv_copied, b * TB)
                        pe.wait_ge(gate_done, b)
                        for i in range(TB):
                            lat = latT[:, i * P:(i + 1) * P]
                            if i >= 2:
                                pe.wait_ge(qkv_copied, b * TB + i - 1)
                            pe.matmul(psQ[:, i % 2, 0:QKV], lat, wall[:, 0:QKV], start=True, stop=True).then_inc(qkv_ready, 1)
                            mm = pe.matmul(psG[:, i, :], lat, wall[:, QKV:QKV + D], start=True, stop=True, skip_group_check=True)
                        mm.then_inc(gate_ready, 1)

        with ExitStack() as inner:
            sb2, ps2, _ = allocators(nc, inner, "decayed")
            t1, t2 = sb2("t1", [P, TB, 2 * D]), sb2("t2", [P, TB, 2 * D])
            rms = sb2("rms", [P, 2, TB * 2 * H0])
            qf, kf = t2[:, :, 0:D], t2[:, :, D:2 * D]
            vf = sb2("vf", [P, TB, H0, V1])
            qkT = sb2("qkT", [P, 2, 2 * P])
            qdiag = sb2("qdiag", [P, H0, P])
            probs = sb2("probs", [P, H0, P])
            state = sb2("state", [P, H0 * V1])
            den = sb2("den", [P, 2, H0])
            o = sb2("o", [P, D])
            osq = sb2("osq", [P, D])
            rmso = sb2("rmso", [P, 2, 2])
            oT = sb2("oT", [P, P])
            y = sb2("y", [P, D])
            psQK = ps2("psQK", [P, 2, 512])
            psS = ps2("psS", [P, H0, P])
            psA = ps2("psA", [P, 512])
            psW = ps2("psW", [P, 512])
            psO = ps2("psO", [P, 512])
            psY = ps2("psY", [P, 512])
            dve_steps, squared, exped, scaled, turned = sem("feature_steps"), sem("squared"), sem("exped"), sem("qk_scaled"), sem("rotated")
            qk_square_ready, qk_root_ready, o_root_ready = sem("qk_square_ready"), sem("qk_root_ready"), sem("o_root_ready")
            features_ready, ones_set = sem("features_ready"), sem("ones_set")
            qkT_ready, qkT_copied, qdiag_set = sem("qkT_ready"), sem("qkT_copied"), sem("qdiag_set")
            scores_ready, probs_ready, state_ready, state_masked = sem("scores_ready"), sem("probs_ready"), sem("state_ready"), sem("state_masked")
            acc_ready, o_ready, oT_ready, oT_copied, y_ready, y_added = (sem(n) for n in (
                "acc_ready", "o_ready", "oT_ready", "oT_copied", "y_ready", "y_added"))

            FSTEPS = 6 + 4 * TB
            with nc.Block() as block:
                @block.gpsimd
                def _(pool):
                    pool.memset(vf[:], 1.0).then_inc(ones_set, 1)
                    pool.memset(qdiag[:], 0.0).then_inc(ones_set, 1)
                    pool.wait_ge(ones_set, 2)
                    with pool.Fori(0, B) as b:
                        pool.wait_ge(qk_square_ready, b + 1)
                        inverse_root(pool, K, rms[:, 0, :], rms[:, 1, :]).then_inc(qk_root_ready, 1)
                        pool.wait_ge(scaled, b + 1)
                        qk = qkv[:, ds(b * TB, TB), 0:2 * D]
                        for j in range(2):
                            xs = qk[:, :, j * D:(j + 1) * D].rearrange("p i (h d) -> p i h d", h=H0)
                            c = rope_c[:, :, j, :]
                            s = rope_s[:, :, j, :]
                            r1 = t1[:, :, j * D:(j + 1) * D].rearrange("p i (h d) -> p i h d", h=H0)
                            r2 = t2[:, :, j * D:(j + 1) * D].rearrange("p i (h d) -> p i h d", h=H0)
                            hw = DH0 // 2
                            pool.tensor_tensor(r1, xs, c[:, :, None, :].to_broadcast([P, TB, H0, DH0]), ALU.mult).then_inc(turned, 1)
                            pool.tensor_tensor(r2[:, :, :, 0:hw], xs[:, :, :, hw:DH0], s[:, :, None, 0:hw].to_broadcast([P, TB, H0, hw]), ALU.mult).then_inc(turned, 1)
                            pool.tensor_tensor(r2[:, :, :, hw:DH0], xs[:, :, :, 0:hw], s[:, :, None, hw:DH0].to_broadcast([P, TB, H0, hw]), ALU.mult).then_inc(turned, 1)
                        for i in range(TB):
                            pool.wait_ge(o_ready, b * TB + i + 1)
                            inverse_root(pool, K, rmso[:, 1, 0:1], rmso[:, 0, 1:2]).then_inc(o_root_ready, 1)

                @block.scalar
                def _(act):
                    with act.Fori(0, B) as b:
                        qk = qkv[:, ds(b * TB, TB), 0:2 * D]
                        act.wait_ge(features_ready, b)
                        act.activation(t1[:], qk, ACT.Square).then_inc(squared, 1)
                        act.wait_ge(dve_steps, b * FSTEPS + 3)
                        act.activation(t1[:], t1[:], ACT.Exp).then_inc(exped, 1)
                        for i in range(TB):
                            g = b * TB + i
                            act.wait_ge(qkT_ready, g + 1)
                            act.activation(qkT[:, i % 2, :], psQK[:, i % 2, 0:2 * P], ACT.Copy).then_inc(qkT_copied, 1)
                            act.wait_ge(scores_ready, g)
                            for h in range(H0):
                                r = slice(h * DH0, (h + 1) * DH0)
                                ins = act.activation(qdiag[r, h, :], psQK[r, i % 2, 0:P], ACT.Copy)
                            ins.then_inc(qdiag_set, 1)
                            act.wait_ge(oT_ready, g + 1)
                            act.activation(oT[:], psO[:, 0:P], ACT.Copy).then_inc(oT_copied, 1)

                @block.vector
                def _(dve):
                    steps = Steps(dve, dve_steps)
                    dve.wait_ge(ones_set, 2)
                    with dve.Fori(0, B) as b:
                        steps.turn(b, FSTEPS)
                        tiles = ds(b * TB, TB)
                        qk = qkv[:, tiles, 0:2 * D]
                        dve.wait_ge(squared, b + 1)
                        steps.then(dve.tensor_reduce(rms[:, 0, :], t1[:].rearrange("p i (g d) -> p (i g) d", d=DH0), X, ALU.add))
                        dve.tensor_scalar(rms[:, 1, :], rms[:, 0, :], 1.0 / DH0, RMS_EPS, ALU.mult, ALU.add).then_inc(qk_square_ready, 1)
                        dve.wait_ge(qk_root_ready, b + 1)
                        heads = qk.rearrange("p i (g d) -> p i g d", d=DH0)
                        dve.tensor_tensor(heads, heads, rms[:, 0, :].rearrange("p (i g) -> p i g", i=TB)[:, :, :, None].to_broadcast([P, TB, 2 * H0, DH0]),
                                          ALU.mult).then_inc(scaled, 1)
                        dve.wait_ge(turned, (b + 1) * 6)
                        steps.then(dve.tensor_tensor(t2[:], t1[:], t2[:], ALU.add))
                        steps.then(dve.tensor_scalar(t1[:], t2[:], 0.0, None, ALU.min))
                        dve.wait_ge(exped, b + 1)
                        steps.then(dve.scalar_tensor_tensor(t1[:], t2[:], 0.0, t1[:], ALU.max, ALU.add))
                        dve.wait_ge(y_ready, b * TB)
                        for j, (dst, scale) in enumerate(((qf, decay), (kf, kscale))):
                            steps.mark(dve.tensor_tensor(dst.rearrange("p i (h d) -> p i h d", h=H0),
                                                         t1[:, :, j * D:(j + 1) * D].rearrange("p i (h d) -> p i h d", h=H0),
                                                         scale[:, :, :, None].to_broadcast([P, TB, H0, DH0]), ALU.mult))
                        dve.tensor_tensor(vf[:, :, :, 0:DH0], qkv[:, tiles, 2 * D:3 * D].rearrange("p i (h d) -> p i h d", h=H0),
                                          gate[:, tiles, :][:, :, :, None].to_broadcast([P, TB, H0, DH0]), ALU.mult).then_inc(features_ready, 1)
                        for i in range(TB):
                            g = b * TB + i
                            dve.wait_ge(scores_ready, g + 1)
                            dve.tensor_tensor(probs[:], psS[:], K.const("causal")[:, None, :].to_broadcast([P, H0, P]), ALU.mult).then_inc(probs_ready, 1)
                            dve.wait_ge(acc_ready, g + 1)
                            acc = psA[:, 0:H0 * V1].rearrange("p (h e) -> p h e", h=H0)
                            steps.then(dve.tensor_scalar(den[:, 0, :], acc[:, :, DH0], 1e-5, None, ALU.max))
                            steps.then(dve.reciprocal(den[:, 1, :], den[:, 0, :]))
                            steps.then(dve.tensor_tensor(o[:].rearrange("p (h d) -> p h d", h=H0), acc[:, :, 0:DH0],
                                                         den[:, 1, :, None].to_broadcast([P, H0, DH0]), ALU.mult))
                            if i < TB - 1:
                                dve.wait_ge(state_ready, b * (TB - 1) + i + 1)
                                dve.tensor_tensor(state[:], psW[:, 0:H0 * V1], K.const("headblock"), ALU.mult).then_inc(state_masked, 1)
                            steps.then(dve.tensor_tensor_reduce(osq[:], o[:], o[:], 1.0, 0.0, ALU.mult, ALU.add, rmso[:, 0, 0:1]))
                            dve.tensor_scalar(rmso[:, 0, 1:2], rmso[:, 0, 0:1], 1.0 / D, RMS_EPS, ALU.mult, ALU.add).then_inc(o_ready, 1)
                            dve.wait_ge(o_root_ready, g + 1)
                            dve.wait_ge(y_ready, g + 1)
                            dve.scalar_tensor_tensor(y[:], psY[:, 0:D], rmso[:, 1, 0:1], gate_out[:, ds(g, 1), :].rearrange("p a d -> p (a d)"),
                                                     ALU.mult, ALU.mult).then_inc(y_added, 1)
                            dve.wait_ge(y_added, 2 * g + 1)
                            row = K.hidden[:, ds(g, 1), :].rearrange("p a d -> p (a d)")
                            dve.tensor_tensor(row, row, y[:], ALU.add).then_inc(y_added, 1)
                    steps.end(B)

                @block.tensor
                def _(pe):
                    def front(b, i):
                        g = b * TB + i
                        pe.transpose(psQK[:, i % 2, 0:P], qf[:, i, :], ident)
                        pe.transpose(psQK[:, i % 2, P:2 * P], kf[:, i, :], ident).then_inc(qkT_ready, 1)
                        if i < TB - 1:
                            if i:
                                pe.wait_ge(state_masked, b * (TB - 1) + i)
                            pe.matmul(psW[:, 0:H0 * V1], kf[:, i, :], vf[:, i].rearrange("p h e -> p (h e)"),
                                      start=(i == 0), stop=True, skip_group_check=True).then_inc(state_ready, 1)

                    def scores(b, i):
                        g = b * TB + i
                        pe.wait_ge(qdiag_set, g + 1)
                        pe.wait_ge(probs_ready, g)
                        pe.matmul(psS[:].rearrange("p h l -> p (h l)"), qkT[:, i % 2, P:2 * P], qdiag[:].rearrange("p h l -> p (h l)"),
                                  start=True, stop=True).then_inc(scores_ready, 1)

                    def back(b, i):
                        g = b * TB + i
                        pe.wait_ge(y_added, 2 * g)
                        if i:
                            pe.wait_ge(state_masked, b * (TB - 1) + i)
                            pe.matmul(psA[:, 0:H0 * V1], qkT[:, i % 2, 0:P], state[:], start=True, stop=False, skip_group_check=True)
                        pe.wait_ge(probs_ready, g + 1)
                        for h in range(H0):
                            mm = pe.matmul(psA[:, h * V1:(h + 1) * V1], probs[:, h, :], vf[:, i, h, :],
                                           start=(i == 0 and h == 0), stop=True, skip_group_check=True)
                        mm.then_inc(acc_ready, 1)
                        pe.wait_ge(o_ready, g + 1)
                        pe.transpose(psO[:, 0:P], o[:], ident).then_inc(oT_ready, 1)
                        pe.wait_ge(oT_copied, g + 1)
                        pe.matmul(psY[:, 0:D], oT[:], wp[:], start=True, stop=True).then_inc(y_ready, 1)

                    with pe.Fori(0, B) as b:
                        pe.wait_ge(features_ready, b + 1)
                        for i in range(TB):
                            front(b, i)
                            scores(b, i)
                            back(b, i)

        clear_semaphores(nc, s_const, y_added)


def route_and_mix(nc, a, K, top, out=None):
    last = top == 2
    if last:
        names = {"router": "L1_ffn_router_w", "w1": "L1_ffn_w1", "b1": "L1_ffn_b1", "w2": "L1_ffn_w2", "b2": "L1_ffn_b2"}
    else:
        names = {"router": "L0_ffn_Wr", "w1": "L0_ffn_W1", "b1": "L0_ffn_b1", "w2": "L0_ffn_W2", "b2": "L0_ffn_b2"}
    tiles = SLOT_TILES[top]
    phase = f"moe{top}"
    with ExitStack() as ctx:
        sb, ps, sem = allocators(nc, ctx, phase)
        ident = K.const("ident")
        w1 = sb("w1", [P, E, F])
        w2 = sb("w2", [P, E, FC, D])
        b1 = sb("b1", [P, FC, E])
        b2 = sb("b2", [P, E, D])
        slots = sb("slots", [P, top, G], U32)
        share = sb("share", [P, 2, G])
        owner = sb("owner", [1, tiles], I32)
        if last:
            gamma, beta = sb("gamma", [P, E, D]), sb("beta", [P, E, D])
        weights_in, bias_set = sem("weights_in"), sem("bias_set")
        weights_landed = 16 * ((3 if last else 2) + 3 + FC)

        with ExitStack() as inner:
            sbr, psr, _ = allocators(nc, inner, phase + "route")
            norm = LayerNorm(nc, inner, phase + "norm")
            normed = sbr("normed", [P, G, D])
            router = sbr("router", [P, E])
            router_bias = sbr("router_bias", [P, E])
            normT = sbr("normT", [P, 2, L])
            logits = sbr("logits", [P, G, E])
            picked = [sbr(f"picked{k}", [P, G, E]) for k in range(top)]
            work, equal = sbr("work", [P, G, E]), sbr("equal", [P, G, E])
            peak = sbr("peak", [P, 2, G])
            picks = sbr("picks", [P, G, E], BF16)
            before, all_ones = sbr("before", [P, P], BF16), sbr("all_ones", [P, P], BF16)
            many = sbr("many", [P, E, G])
            count, first, end = sbr("count", [P, E]), sbr("first", [P, E]), sbr("end", [P, E])
            pairs = sbr("pairs", [P, E, E])
            place = sbr("place", [P, G])
            passed = sbr("passed", [1, tiles, E])
            tile_expert = sbr("tile_expert", [1, tiles])
            psT = psr("psT", [P, 2, L])
            psR = psr("psR", [P, 2, 512])
            psC, psN = psr("psC", [P, 512]), psr("psN", [P, 512])
            peaks_apart = sem("peaks_apart")
            norm_ready, normT_ready, normT_copied, rows_kept = sem("norm_ready"), sem("normT_ready"), sem("normT_copied"), sem("rows_kept")
            logits_ready, logits_done, route_steps = sem("logits_ready"), sem("logits_done"), sem("route_steps")
            picks_ready, ranks_ready, gates_exped, slots_ready, routed = (sem(n) for n in (
                "picks_ready", "ranks_ready", "gates_exped", "slots_ready", "routed"))

            with nc.Block() as block:
                @block.sync
                def _(sp):
                    sp.dma_start(router[:], a[names["router"]]).then_inc(weights_in, 16)
                    if last:
                        sp.dma_start(gamma[:].rearrange("p e d -> p (e d)"), everywhere(a["L1_ffn_gamma"].rearrange("e d -> (e d)"), E * D)).then_inc(weights_in, 16)
                        sp.dma_start(beta[:].rearrange("p e d -> p (e d)"), everywhere(a["L1_ffn_beta"].rearrange("e d -> (e d)"), E * D)).then_inc(weights_in, 16)
                    else:
                        sp.dma_start(router_bias[:], everywhere(a["L0_ffn_br"], E)).then_inc(weights_in, 16)
                    sp.dma_start(w1[:], a[names["w1"]].rearrange("e d f -> d e f")).then_inc(weights_in, 16)
                    sp.dma_start(w2[:], a[names["w2"]].rearrange("e (c p) d -> p e c d", p=P)).then_inc(weights_in, 16)
                    sp.dma_start(b2[:].rearrange("p e d -> p (e d)"), everywhere(a[names["b2"]].rearrange("e d -> (e d)"), E * D)).then_inc(weights_in, 16)
                    for c in range(FC):
                        sp.dma_start(b1[:, c, :], a[names["b1"]][:, c * P:(c + 1) * P].rearrange("e p -> p e"),
                                     allow_slow_non_contiguous=True).then_inc(weights_in, 16)

                @block.scalar
                def _(act):
                    with act.Fori(0, B // 2) as it:
                        for s in range(2):
                            b = it * 2 + s
                            act.wait_ge(normT_ready, b + 1)
                            act.activation(normT[:, s, :], psT[:, s, :], ACT.Copy).then_inc(normT_copied, 1)
                            act.activation(normed[:, ds(b * TB, TB), :], norm.rows[:], ACT.Copy).then_inc(rows_kept, 1)
                    if last:
                        act.wait_ge(peaks_apart, 1)
                        act.activation(share[:, 1, :], share[:, 0, :], ACT.Exp).then_inc(gates_exped, 1)

                @block.gpsimd
                def _(pool):
                    with pool.Fori(0, B) as b:
                        norm.on_pool(pool, K, b, norm_ready)
                    pool.wait_ge(slots_ready, top)
                    pool.wait_ge(rows_kept, B)
                    for k in range(top):
                        for g in range(G):
                            pool.indirect_dma_start(K.routed_dram[top], bass.IndirectOffsetOnAxis(ap=slots[:, k, g:g + 1], axis=0),
                                                    normed[:, g, :], None).then_inc(routed, 16)
                    pool.wait_ge(routed, 16 * top * G)

                @block.tensor
                def _(pe):
                    pe.wait_ge(weights_in, weights_landed)
                    with pe.Fori(0, B // 2) as it:
                        for s in range(2):
                            b = it * 2 + s
                            pe.wait_ge(norm_ready, b + 1)
                            for i in range(TB):
                                mm = pe.transpose(psT[:, s, i * P:(i + 1) * P], norm.rows[:, i, :], ident)
                            mm.then_inc(normT_ready, 1)
                            pe.wait_ge(normT_copied, b + 1)
                            pe.wait_ge(logits_done, it * 2)
                            for i in range(TB):
                                mm = pe.matmul(psR[:, s, i * E:(i + 1) * E], normT[:, s, i * P:(i + 1) * P], router[:], start=True, stop=True,
                                               skip_group_check=True)
                            mm.then_inc(logits_ready, 1)
                    pe.wait_ge(picks_ready, 1)
                    pe.matmul(psC[:, 0:G * E], before[:], picks[:].rearrange("p g e -> p (g e)"), start=True, stop=False, skip_group_check=True)
                    for g in range(G - 1):
                        pe.matmul(psC[:, (g + 1) * E:G * E].rearrange("p (g e) -> p g e", e=E), all_ones[:],
                                  picks[:, g:g + 1, :].to_broadcast([P, G - 1 - g, E]), start=False, stop=(g == G - 2), skip_group_check=True)
                    for g in range(G):
                        mm = pe.matmul(psN[:, 0:E], all_ones[:], picks[:, g, :], start=(g == 0), stop=(g == G - 1))
                    mm.then_inc(ranks_ready, 1)

                @block.vector
                def _(dve):
                    if last:
                        dve.memset(router_bias[:], 0.0).then_inc(bias_set, 1)
                        dve.wait_ge(bias_set, 1)
                    dve.wait_ge(weights_in, weights_landed)
                    steps = Steps(dve, norm.steps)

                    def collect(b, s):
                        dve.wait_ge(logits_ready, b + 1)
                        dve.tensor_tensor(logits[:, ds(b * TB, TB), :], psR[:, s, 0:TB * E].rearrange("p (i e) -> p i e", e=E),
                                          router_bias[:, None, :].to_broadcast([P, TB, E]), ALU.add).then_inc(logits_done, 1)

                    with dve.Fori(0, B // 2) as it:
                        steps.turn(it, 2 * norm.marks)
                        for s in range(2):
                            b = it * 2 + s
                            dve.wait_ge(rows_kept, b)
                            norm.on_vector(dve, steps, b, K.hidden, normT_ready, norm_ready)
                            collect(b, s)
                    steps.end(B // 2)
                    dve.wait_ge(logits_done, B)

                    steps = Steps(dve, route_steps)

                    def per_tile(ap):
                        return ap[:, :, None].to_broadcast([P, G, E])

                    scores = logits
                    for k in range(top):
                        steps.then(dve.tensor_reduce(peak[:, k, :], scores[:], X, ALU.max))
                        steps.then(dve.tensor_tensor(equal[:], scores[:], per_tile(peak[:, k, :]), ALU.is_equal))
                        steps.then(dve.tensor_tensor(equal[:], equal[:], K.const("descend")[:, None, :].to_broadcast([P, G, E]), ALU.mult))
                        steps.then(dve.tensor_reduce(place[:], equal[:], X, ALU.max))
                        steps.then(dve.tensor_tensor(picked[k][:], equal[:], per_tile(place[:]), ALU.is_equal))
                        if k < top - 1:
                            steps.then(dve.scalar_tensor_tensor(work[:], picked[k][:], -BIG, logits[:], ALU.mult, ALU.add))
                            scores = work
                    if last:
                        dve.tensor_tensor(share[:, 0, :], peak[:, 1, :], peak[:, 0, :], ALU.subtract).then_inc(peaks_apart, 1)
                    steps.mark(dve.tensor_copy(before[:], K.const("before")))
                    steps.mark(dve.memset(all_ones[:], 1.0))
                    steps.wait()
                    if last:
                        dve.tensor_tensor(picks[:], picked[0][:], picked[1][:], ALU.add).then_inc(picks_ready, 1)
                        dve.wait_ge(gates_exped, 1)
                        steps.then(dve.tensor_scalar(place[:], share[:, 1, :], 1.0, None, ALU.add))
                        steps.then(dve.reciprocal(share[:, 0, :], place[:]))
                        steps.then(dve.tensor_tensor(share[:, 1, :], share[:, 1, :], share[:, 0, :], ALU.mult))
                    else:
                        dve.tensor_copy(picks[:], picked[0][:]).then_inc(picks_ready, 1)
                    dve.wait_ge(ranks_ready, 1)
                    steps.then(dve.tensor_tensor(many[:], psN[:, 0:E, None].to_broadcast([P, E, G]),
                                                 K.const("tiles128")[:, None, :].to_broadcast([P, E, G]), ALU.is_gt))
                    steps.then(dve.tensor_reduce(count[:], many[:], X, ALU.add))
                    steps.then(dve.tensor_tensor(pairs[:], count[:, None, :].to_broadcast([P, E, E]),
                                                 K.const("earlier").rearrange("p (e f) -> p e f", e=E), ALU.mult))
                    steps.then(dve.tensor_reduce(first[:], pairs[:], X, ALU.add))
                    steps.then(dve.tensor_tensor(end[:], first[:], count[:], ALU.add))
                    steps.then(dve.tensor_scalar(first[:], first[:], float(P), None, ALU.mult))
                    steps.then(dve.tensor_tensor(work[:], psC[:, 0:G * E].rearrange("p (g e) -> p g e", e=E),
                                                 first[:, None, :].to_broadcast([P, G, E]), ALU.add))
                    for k in range(top):
                        steps.then(dve.tensor_tensor(equal[:], picked[k][:], work[:], ALU.mult))
                        steps.then(dve.tensor_reduce(place[:], equal[:], X, ALU.add))
                        dve.tensor_copy(slots[:, k, :], place[:]).then_inc(slots_ready, 1)
                        dve.wait_ge(slots_ready, k + 1)
                    steps.then(dve.tensor_tensor(passed[:], K.const("slot")[0:1, 0:tiles, None].to_broadcast([1, tiles, E]),
                                                 end[0:1, None, :].to_broadcast([1, tiles, E]), ALU.is_ge))
                    steps.then(dve.tensor_reduce(tile_expert[:], passed[:], X, ALU.add))
                    steps.then(dve.tensor_scalar(tile_expert[:], tile_expert[:], float(E - 1), None, ALU.min))
                    steps.then(dve.tensor_copy(owner[:], tile_expert[:]))

        with ExitStack() as inner:
            sbe, pse, _ = allocators(nc, inner, phase + "mix")
            RING, PAIR = 8, 2
            rows = sbe("rows", [P, RING, D])
            rowsT = sbe("rowsT", [P, 2, P])
            hid = sbe("hid", [P, 2, F])
            hidT = sbe("hidT", [P, 2, F])
            result = sbe("result", [P, RING, D])
            stats, mv = sbe("stats", [P, 6]), sbe("mv", [P, 2])
            square, root, pause = sbe("square", [P, 1]), sbe("root", [P, 1]), sbe("pause", [P, 1])
            psX = pse("psX", [P, 512])
            psH, psF, psY = pse("psH", [P, 2, F]), pse("psF", [P, 2, F]), pse("psY", [P, 2, 512])
            rows_in = [sem(f"rows_in{i}") for i in range(RING // PAIR)]
            result_out = [sem(f"result_out{i}") for i in range(RING // PAIR)]
            rowsT_ready, rowsT_copied = sem("rowsT_ready"), sem("rowsT_copied")
            hid_ready, hid_copied, hidT_ready, hidT_done = sem("hid_ready"), sem("hid_copied"), sem("hidT_ready"), sem("hidT_done")
            mixed_ready, result_ready, mix_steps = sem("mixed_ready"), sem("result_ready"), sem("mix_steps")
            square_ready, root_ready = sem("mix_square_ready"), sem("mix_root_ready")
            turns = tiles // RING
            MARKS = 6 if last else 0

            def slot_rows(ap, t):
                return ap[ds(t * P, PAIR * P), :].rearrange("(n p) d -> p n d", p=P)

            def expert(engine, t):
                return engine.value_load(owner[0:1, ds(t, 1)], min_val=0, max_val=E - 1)

            def experts(engine, first, n):
                return [expert(engine, first + k) for k in range(n)]

            with nc.Block() as block:
                @block.sync
                def _(sp):
                    def load(t, s):
                        sp.dma_start(rows[:, s:s + PAIR, :], slot_rows(K.routed_dram[top], t)).then_inc(rows_in[s // PAIR], 16)

                    read = result_ready if last else rowsT_ready
                    for s in range(0, RING, PAIR):
                        load(s, s)
                    with sp.Fori(1, turns) as it:
                        for s in range(0, RING, PAIR):
                            sp.wait_ge(read, (it - 1) * RING + s + PAIR)
                            load(it * RING + s, s)

                @block.gpsimd
                def _(pool):
                    with pool.Fori(0, turns) as it:
                        for s in range(RING):
                            t = it * RING + s
                            if last:
                                pool.wait_ge(square_ready, t + 1)
                                pool.wait_ge(result_ready, t)
                                inverse_root(pool, K, root[:], square[:]).then_inc(root_ready, 1)
                            if s % PAIR == PAIR - 1:
                                s0 = s - PAIR + 1
                                pool.wait_ge(result_ready, t + 1)
                                pool.dma_start(slot_rows(K.result_dram[top], it * RING + s0), result[:, s0:s0 + PAIR, :]).then_inc(result_out[s // PAIR], 16)
                    for n in range(RING // PAIR):
                        pool.wait_ge(result_out[n], 16 * turns)

                @block.tensor
                def _(pe):
                    def first_product(t, s, e):
                        pe.matmul(psH[:, s % 2, :], rowsT[:, s % 2, :], w1[:].rearrange("p e f -> p (e f)")[:, ds(e * F, F)],
                                  start=True, stop=True).then_inc(hid_ready, 1)

                    def turn_rows(s, turn):
                        pe.wait_ge(rows_in[s // PAIR], (turn + 1) * 16)
                        pe.transpose(psX[:, 0:P], rows[:, s, :], ident).then_inc(rowsT_ready, 1)

                    def turn_hidden(t, s):
                        pe.wait_ge(hid_copied, t + 1)
                        for c in range(FC):
                            mm = pe.transpose(psF[:, s % 2, c * P:(c + 1) * P], hid[:, s % 2, c * P:(c + 1) * P], ident)
                        mm.then_inc(hidT_ready, 1)

                    def second_product(t, s, e, bank_used):
                        pe.wait_ge(hidT_done, t + 1)
                        if bank_used:
                            pe.wait_ge(result_ready, t - 1)
                        for c in range(FC):
                            mm = pe.matmul(psY[:, s % 2, 0:D], hidT[:, s % 2, c * P:(c + 1) * P],
                                           w2[:].rearrange("p e c d -> p (e c d)")[:, ds(e * (FC * D) + c * D, D)],
                                           start=(c == 0), stop=(c == FC - 1))
                        mm.then_inc(mixed_ready, 1)

                    def turn(first, it, opening, closing):
                        begin = 0 if opening else -2
                        e = dict(zip(range(begin, RING), experts(pe, first + begin, RING - begin)))
                        for s in range(RING):
                            t = first + s
                            pe.wait_ge(rowsT_copied, t + 1)
                            if s < RING - 1:
                                turn_rows(s + 1, it)
                            elif not closing:
                                turn_rows(0, it + 1)
                            first_product(t, s, e[s])
                            if s >= 1 or not opening:
                                turn_hidden(t - 1, (s + 1) % 2)
                            if s >= 2 or not opening:
                                second_product(t - 2, s % 2, e[s - 2], s >= 4 or not opening)
                        return e

                    pe.wait_ge(weights_in, weights_landed)
                    turn_rows(0, 0)
                    turn(0, 0, True, False)
                    with pe.Fori(1, turns - 1) as it:
                        turn(it * RING, it, False, False)
                    e = turn((turns - 1) * RING, turns - 1, False, True)
                    turn_hidden(tiles - 1, 1)
                    second_product(tiles - 2, 0, e[RING - 2], True)
                    second_product(tiles - 1, 1, e[RING - 1], True)

                @block.scalar
                def _(act):
                    def rows_copy(t, s):
                        act.wait_ge(rowsT_ready, t + 1)
                        act.activation(rowsT[:, s % 2, :], psX[:, 0:P], ACT.Copy).then_inc(rowsT_copied, 1)

                    def activate(t, s, e):
                        act.wait_ge(hidT_ready, t + 1)
                        flat = b1[:].rearrange("p c e -> p (c e)")
                        for c in range(FC):
                            ins = act.activation(hidT[:, s % 2, c * P:(c + 1) * P], psF[:, s % 2, c * P:(c + 1) * P], ACT.Relu,
                                                 bias=flat[:, ds(e + c * E, 1)])
                        ins.then_inc(hidT_done, 1)

                    act.wait_ge(weights_in, weights_landed)
                    e = experts(act, 0, RING - 2)
                    rows_copy(0, 0)
                    rows_copy(1, 1)
                    for s in range(2, RING):
                        rows_copy(s, s)
                        activate(s - 2, s, e[s - 2])
                    with act.Fori(1, turns) as it:
                        e = experts(act, it * RING - 2, RING)
                        for s in range(RING):
                            rows_copy(it * RING + s, s)
                            activate(it * RING + s - 2, s, e[s])
                    e = experts(act, tiles - 2, 2)
                    activate(tiles - 2, 0, e[0])
                    activate(tiles - 1, 1, e[1])

                @block.vector
                def _(dve):
                    steps = Steps(dve, mix_steps)

                    def hidden_copy(t, s):
                        dve.wait_ge(hid_ready, t + 1)
                        dve.tensor_copy(hid[:, s % 2, :], psH[:, s % 2, :]).then_inc(hid_copied, 1)

                    def of_expert(table, e):
                        return table[:].rearrange("p e d -> p (e d)")[:, ds(e * D, D)]

                    def finish(t, s, it, e):
                        dve.wait_ge(result_out[s // PAIR], it * 16)
                        res, mixed = result[:, s, :], psY[:, s % 2, 0:D]
                        if not last:
                            dve.wait_ge(mixed_ready, t + 1)
                            dve.tensor_tensor(res, mixed, of_expert(b2, e), ALU.add).then_inc(result_ready, 1)
                            return
                        steps.then(dve.tensor_tensor(res, rows[:, s, :], of_expert(b2, e), ALU.add))
                        dve.wait_ge(mixed_ready, t + 1)
                        steps.then(dve.tensor_tensor(res, mixed, res, ALU.add))
                        steps.mark(dve.bn_stats(stats[:], res))
                        steps.wait_apart(pause[:])
                        steps.then(dve.bn_aggr(mv[:], stats[:]))
                        dve.tensor_scalar(square[:], mv[:, 1:2], RMS_EPS, None, ALU.add).then_inc(square_ready, 1)
                        dve.wait_ge(root_ready, t + 1)
                        steps.then(dve.tensor_scalar(res, res, mv[:, 0:1], root[:], ALU.subtract, ALU.mult))
                        steps.then(dve.tensor_tensor(res, res, of_expert(gamma, e), ALU.mult))
                        dve.tensor_tensor(res, res, of_expert(beta, e), ALU.add).then_inc(result_ready, 1)

                    dve.wait_ge(weights_in, weights_landed)
                    e = experts(dve, 0, RING - 2)
                    hidden_copy(0, 0)
                    hidden_copy(1, 1)
                    for s in range(2, RING):
                        hidden_copy(s, s)
                        finish(s - 2, s - 2, 0, e[s - 2])
                    with dve.Fori(1, turns) as it:
                        steps.turn(it - 1, RING * MARKS)
                        e = experts(dve, it * RING - 2, RING)
                        for s in range(RING):
                            t = it * RING + s
                            hidden_copy(t, s)
                            finish(t - 2, (s - 2) % RING, it - 1 if s < 2 else it, e[s])
                    steps.end(turns - 1)
                    e = experts(dve, tiles - 2, 2)
                    finish(tiles - 2, RING - 2, turns - 1, e[0])
                    finish(tiles - 1, RING - 1, turns - 1, e[1])

        with ExitStack() as inner:
            sbb, _, _ = allocators(nc, inner, phase + "back")
            back = sbb("back", [P, top, G, D])
            taken = [[sem(f"taken{k}_{q}") for q in range(2)] for k in range(top)]
            added, stored = sem("added"), sem("stored")
            QT = G // 2
            with nc.Block() as block:
                @block.gpsimd
                def _(pool):
                    for g in range(G):
                        for k in range(top):
                            pool.indirect_dma_start(back[:, k, g, :], None, K.result_dram[top],
                                                    bass.IndirectOffsetOnAxis(ap=slots[:, k, g:g + 1], axis=0)).then_inc(taken[k][g // QT], 16)

                @block.vector
                def _(dve):
                    steps = 0
                    for q in range(2):
                        half = slice(q * QT, (q + 1) * QT)
                        rows = K.hidden[:, half, :]
                        for k in range(top):
                            dve.wait_ge(taken[k][q], 16 * QT)
                            part = back[:, k, half, :]
                            if last:
                                dve.tensor_tensor(part, part, share[:, k, half, None].to_broadcast([P, QT, D]), ALU.mult).then_inc(added, 1)
                                steps += 1
                                dve.wait_ge(added, steps)
                            dve.tensor_tensor(rows, rows, part, ALU.add).then_inc(added, 1)
                            steps += 1
                            dve.wait_ge(added, steps)

                if last:
                    @block.sync
                    def _(sp):
                        rows_out = out.rearrange("b (i p) d -> p (b i) d", p=P)
                        for q in range(2):
                            sp.wait_ge(added, 4 * (q + 1))
                            sp.dma_start(rows_out[:, q * QT:(q + 1) * QT, :], K.hidden[:, q * QT:(q + 1) * QT, :]).then_inc(stored, 16)
                        sp.wait_ge(stored, 32)


def cross_attention(nc, a, K):
    with ExitStack() as ctx:
        sb, ps, sem = allocators(nc, ctx, "cross")
        ident = K.const("ident")
        qT = sb("normT", [P, (B + 1) * L])
        mixed = sb("mixed", [P, G, D])
        norm_ready, normT_ready, normT_copied = sem("norm_ready"), sem("normT_ready"), sem("normT_copied")

        with ExitStack() as inner:
            sbn, psn, _ = allocators(nc, inner, "crossnorm")
            norm = LayerNorm(nc, inner, "crossnorm")
            psT = psn("psT", [P, 2, L])
            tail_set = sem("tail_set")
            with nc.Block() as block:
                @block.vector
                def _(dve):
                    dve.memset(qT[:, B * L:(B + 1) * L], 0.0).then_inc(tail_set, 1)
                    steps = Steps(dve, norm.steps)
                    with dve.Fori(0, B) as b:
                        steps.turn(b, norm.marks)
                        norm.on_vector(dve, steps, b, K.hidden, normT_ready, norm_ready)
                    steps.end(B)

                @block.gpsimd
                def _(pool):
                    with pool.Fori(0, B) as b:
                        norm.on_pool(pool, K, b, norm_ready)

                @block.tensor
                def _(pe):
                    with pe.Fori(0, B // 2) as it:
                        for s in range(2):
                            b = it * 2 + s
                            pe.wait_ge(norm_ready, b + 1)
                            pe.wait_ge(normT_copied, it * 2)
                            for i in range(TB):
                                mm = pe.transpose(psT[:, s, i * P:(i + 1) * P], norm.rows[:, i, :], ident)
                            mm.then_inc(normT_ready, 1)

                @block.scalar
                def _(act):
                    with act.Fori(0, B // 2) as it:
                        for s in range(2):
                            b = it * 2 + s
                            act.wait_ge(normT_ready, b + 1)
                            act.activation(qT[:, ds(b * L, L)], psT[:, s, :], ACT.Copy).then_inc(normT_copied, 1)

        with ExitStack() as inner:
            sba, psa, _ = allocators(nc, inner, "attend")
            q_high = [sba(f"q_high{h}", [P, L], F32R) for h in range(H1)]
            q_low = [sba(f"q_low{h}", [P, L], F32R) for h in range(H1)]
            maxima = sba("maxima", [P, TB, VC], F32R)
            weights = sba("weights", [P, TB, KC])
            sums, scales = sba("sums", [P, TB, VC]), sba("scales", [P, TB, VC])
            weightsT = sba("weightsT", [P, 2, KC])
            zero = sba("zero", [1, TB * DH1])
            psL, psT = psa("psL", [P, TB, KC]), psa("psT", [P, 2, KC])
            psA = psa("psA", [P, H1, TB, DH1])
            psQ = psa("psQ", [P, L])
            zero_set, q_ready, q_highs, q_lows = sem("zero_set"), sem("q_ready"), sem("q_highs"), sem("q_lows")
            logits_ready, maxima_ready, shifted, exped = sem("logits_ready"), sem("maxima_ready"), sem("shifted"), sem("exped")
            summed, scales_ready, normalised = sem("summed"), sem("scales_ready"), sem("normalised")
            transposed, copied, run_ready, run_copied = sem("transposed"), sem("copied"), sem("run_ready"), sem("run_copied")

            def runs(engine, run):
                with engine.Fori(0, B) as b:
                    for h in range(H1):
                        run(b, h)

            def unit(b, h, c):
                return ((b * H1 + h) * NKC + c) * TB

            def videos(ap):
                return ap.rearrange("p (v f) -> p v f", f=FR)

            with nc.Block() as block:
                @block.tensor
                def _(pe):
                    def project(h, cols):
                        pe.matmul(psQ[:], K.wq2[:, h, :], qT[:, cols], start=True, stop=True).then_inc(q_ready, 1)

                    def logits(h, s, key):
                        tile = slice(s * P, (s + 1) * P)
                        pe.matmul(psL[:, s, :], q_high[h][:, tile], K.keys[:, ds(key, KC)], start=True, stop=False, skip_group_check=True)
                        pe.matmul(psL[:, s, :], q_low[h][:, tile], K.keys[:, ds(key, KC)], start=False, stop=False,
                                  skip_group_check=True).then_inc(logits_ready, 1)

                    def shift(s):
                        pe.matmul(videos(psL[:, s, :]), K.neg_ident[:], maxima[:, s, :, None].to_broadcast([P, VC, FR]),
                                  start=False, stop=True, skip_group_check=True).then_inc(shifted, 1)

                    def mix(h, s, tile):
                        flat = K.values[:, h].rearrange("p t e -> p (t e)")
                        for k in range(SUB):
                            mm = pe.matmul(psA[:, h, s, :], weightsT[:, s % 2, k * P:(k + 1) * P], flat[:, ds((tile + k) * DH1, DH1)],
                                           start=False, stop=(k == SUB - 1), skip_group_check=True)
                        return mm

                    def step(u, s, head, key, earlier):
                        pe.wait_ge(normalised, u + 1)
                        for k in range(SUB):
                            mm = pe.transpose(psT[:, s % 2, k * P:(k + 1) * P], weights[:, s, k * P:(k + 1) * P], ident)
                        mm.then_inc(transposed, 1)
                        logits(head, s, key)
                        pe.wait_ge(maxima_ready, u + 4)
                        shift((s + 3) % TB)
                        if earlier:
                            pe.wait_ge(copied, u)
                            mix(*earlier)

                    pe.wait_ge(zero_set, 1)
                    project(0, slice(0, L))
                    pe.wait_ge(q_highs, 1)
                    pe.wait_ge(q_lows, 1)
                    for s in range(TB):
                        logits(0, s, 0)
                    for s in range(TB - 1):
                        pe.wait_ge(maxima_ready, s + 1)
                        shift(s)

                    def run(b, h):
                        for s in range(TB):
                            step(unit(b, h, 0) + s, s, h, h * KEYS + KC, (h, s - 1, 0) if s else None)
                            if s == 0:
                                project(1 - h, ds((b + h) * L, L))
                                pe.wait_ge(run_copied, b * H1 + h)
                                pe.matmul(psA[:, h].rearrange("p t e -> p (t e)"), zero[0:1, 0:P], zero[:], start=True, stop=False,
                                          skip_group_check=True)
                        with pe.Fori(1, NKC - 1) as c:
                            for s in range(TB):
                                step(unit(b, h, c) + s, s, h, h * KEYS + (c + 1) * KC,
                                     (h, s - 1, c * SUB) if s else (h, TB - 1, (c - 1) * SUB))
                        pe.wait_ge(q_highs, b * H1 + h + 2)
                        pe.wait_ge(q_lows, b * H1 + h + 2)
                        c = NKC - 1
                        for s in range(TB):
                            step(unit(b, h, c) + s, s, 1 - h, (1 - h) * KEYS,
                                 (h, s - 1, c * SUB) if s else (h, TB - 1, (c - 1) * SUB))
                        pe.wait_ge(copied, unit(b, h, NKC))
                        mix(h, TB - 1, c * SUB).then_inc(run_ready, 1)

                    runs(pe, run)

                @block.vector
                def _(dve):
                    dve.memset(zero[:], 0.0).then_inc(zero_set, 1)

                    def low(h, n):
                        dve.wait_ge(q_highs, n)
                        dve.scalar_tensor_tensor(q_low[h][:], psQ[:], K.bq2[:, h:h + 1], q_high[h][:].bitcast(F32),
                                                 ALU.add, ALU.subtract).then_inc(q_lows, 1)

                    def maximum(s, u):
                        dve.wait_ge(logits_ready, u + 1)
                        dve.tensor_reduce(maxima[:, s, :], videos(psL[:, s, :]), X, ALU.max).then_inc(maxima_ready, 1)

                    def total(s, u):
                        dve.wait_ge(exped, u + 1)
                        dve.tensor_reduce(sums[:, s, :], videos(weights[:, s, :]), X, ALU.add).then_inc(summed, 1)

                    def reciprocal(s, u):
                        dve.wait_ge(summed, u + 1)
                        dve.reciprocal(scales[:, s, :], sums[:, s, :]).then_inc(scales_ready, 1)

                    def step(u, s):
                        maximum(s, u + 4)
                        reciprocal((s + 2) % TB, u + 2)
                        total((s + 3) % TB, u + 3)

                    low(0, 1)
                    maximum(0, 0)
                    maximum(1, 1)
                    total(0, 0)
                    maximum(2, 2)
                    reciprocal(0, 0)
                    total(1, 1)
                    maximum(3, 3)
                    reciprocal(1, 1)
                    total(2, 2)

                    def run(b, h):
                        for s in range(TB):
                            step(unit(b, h, 0) + s, s)
                            if s == 1:
                                low(1 - h, b * H1 + h + 2)
                        with dve.Fori(1, NKC) as c:
                            for s in range(TB):
                                step(unit(b, h, c) + s, s)

                    runs(dve, run)

                @block.scalar
                def _(act):
                    def high(h, n):
                        act.wait_ge(q_ready, n)
                        act.activation(q_high[h][:], psQ[:], ACT.Identity, bias=K.bq2[:, h:h + 1]).then_inc(q_highs, 1)

                    def exponential(s, u):
                        act.wait_ge(shifted, u + 1)
                        act.activation(weights[:, s, :], psL[:, s, :], ACT.Exp, scale=float(DH1) ** -0.5).then_inc(exped, 1)

                    def copy(s, u):
                        act.wait_ge(transposed, u + 1)
                        act.activation(weightsT[:, s % 2, :], psT[:, s % 2, :], ACT.Copy).then_inc(copied, 1)

                    def step(u, s):
                        copy(s, u)
                        exponential((s + 3) % TB, u + 3)

                    high(0, 1)
                    for s in range(TB - 1):
                        exponential(s, s)

                    def run(b, h):
                        for s in range(TB):
                            step(unit(b, h, 0) + s, s)
                            if s == 0:
                                high(1 - h, b * H1 + h + 2)
                        with act.Fori(1, NKC) as c:
                            for s in range(TB):
                                step(unit(b, h, c) + s, s)
                        act.wait_ge(run_ready, b * H1 + h + 1)
                        act.activation(mixed[:, ds(b * TB, TB), h * DH1:(h + 1) * DH1], psA[:, h], ACT.Copy,
                                       scale=1.0 / VID).then_inc(run_copied, 1)

                    runs(act, run)

                @block.gpsimd
                def _(pool):
                    with pool.Fori(0, B * H1 * NKC) as n:
                        for s in range(TB):
                            pool.wait_ge(scales_ready, n * TB + s + 1)
                            w = videos(weights[:, s, :])
                            pool.tensor_tensor(w, w, scales[:, s, :, None].to_broadcast([P, VC, FR]), ALU.mult).then_inc(normalised, 1)

        with ExitStack() as inner:
            sbo, pso, _ = allocators(nc, inner, "crossout")
            mixedT = sbo("mixedT", [P, 2, 2, L // 2])
            psT, psY = pso("psT", [P, 2, L]), pso("psY", [P, 2, H1, 512])
            bias_added, mixedT_ready, mixedT_copied, out_ready, out_added = (sem(n) for n in (
                "bias_added", "mixedT_ready", "mixedT_copied", "out_ready", "out_added"))
            stage = sbo("stage", [P, 2, TB, D])
            staged = sem("staged")
            with nc.Block() as block:
                @block.gpsimd
                def _(pool):
                    with pool.Fori(0, B // 2) as it:
                        for s in range(2):
                            b = it * 2 + s
                            pool.wait_ge(mixedT_ready, it * 2)
                            pool.tensor_copy(stage[:, s], mixed[:, ds(b * TB, TB), :]).then_inc(staged, 1)
                            rows = K.hidden[:, ds(b * TB, TB), :]
                            pool.tensor_tensor(rows, rows, K.bo_all[:, None, :].to_broadcast([P, TB, D]), ALU.add).then_inc(bias_added, 1)

                @block.tensor
                def _(pe):
                    with pe.Fori(0, B // 2) as it:
                        for s in range(2):
                            b = it * 2 + s
                            pe.wait_ge(staged, b + 1)
                            for i in range(TB):
                                mm = pe.transpose(psT[:, s, i * P:(i + 1) * P], stage[:, s, i, :], ident)
                            mm.then_inc(mixedT_ready, 1)
                            pe.wait_ge(mixedT_copied, b + 1)
                            pe.wait_ge(out_added, it * 2)
                            for i in range(TB):
                                h, m = i // (TB // H1), i % (TB // H1)
                                head = slice(h * DH1, (h + 1) * DH1)
                                for side in range(2):
                                    mm = pe.matmul(psY[:, s, h, m * D:(m + 1) * D], mixedT[head, s, side, m * P:(m + 1) * P], K.wo2[head, side, :],
                                                   start=(side == 0), stop=(side == 1), skip_group_check=True)
                            mm.then_inc(out_ready, 1)

                @block.scalar
                def _(act):
                    with act.Fori(0, B // 2) as it:
                        for s in range(2):
                            act.wait_ge(mixedT_ready, it * 2 + s + 1)
                            act.activation(mixedT[:, s], psT[:, s, :].rearrange("p (r side) -> p side r", side=2), ACT.Copy).then_inc(mixedT_copied, 1)

                @block.vector
                def _(dve):
                    with dve.Fori(0, B // 2) as it:
                        for s in range(2):
                            b = it * 2 + s
                            dve.wait_ge(bias_added, b + 1)
                            dve.wait_ge(out_ready, b + 1)
                            rows = K.hidden[:, ds(b * TB, TB), :].rearrange("p (h m) d -> p h (m d)", h=H1)
                            dve.tensor_tensor(rows, rows, psY[:, s, :, 0:TB // H1 * D], ALU.add).then_inc(out_added, 1)


def audio_tower(nc, a, out):
    with ExitStack() as ctx:
        K = Kept(nc, ctx, a)
        select_and_project(nc, a, K)
        retention(nc, a, K)
        route_and_mix(nc, a, K, 1)
        cross_attention(nc, a, K)
        route_and_mix(nc, a, K, 2, out)


_OUT = ((B, L, D), "float32")


def kernel(**inputs):
    import numpy as _np
    import concourse.bacc as _bacc
    from concourse import mybir as _mybir
    from concourse.bass_utils import run_bass_kernel_spmd as _run

    nc = _bacc.Bacc("TRN2", target_bir_lowering=False, num_devices=1)
    arrays, aps = {}, {}
    for name, value in {**inputs, "shape_constants": CONSTANTS}.items():
        value = _np.ascontiguousarray(value)
        arrays[f"in_{name}_dram"] = value
        aps[name] = nc.dram_tensor(f"in_{name}_dram", value.shape, _mybir.dt.from_np(value.dtype), kind="ExternalInput").ap()
    out = nc.dram_tensor("out_0_dram", _OUT[0], _mybir.dt.from_np(_np.dtype(_OUT[1])), kind="ExternalOutput").ap()
    audio_tower(nc, aps, out)
    r = _run(nc, [arrays], core_ids=[0])
    return r.results[0]["out_0_dram"]
```

```python
from contextlib import ExitStack

import numpy as np

import concourse.bass as bass
from concourse import mybir

F32 = mybir.dt.float32
F32R = mybir.dt.float32r
BF16 = mybir.dt.bfloat16
I32 = mybir.dt.int32
U32 = mybir.dt.uint32
ALU = mybir.AluOpType
ACT = mybir.ActivationFunctionType
X = mybir.AxisListType.X
ds = bass.ds

P = 128
B, S, D = 8, 4096, 128
BLOCK, TOP = 128, 16
L = S // BLOCK * TOP
N = B * L
G = N // P
TB = L // P
LAT, H0, DH0 = 64, 4, 32
V1 = DH0 + 1
QKV = 3 * D + 4 * H0
E, F = 8, 512
FC = F // P
VID, FR, H1, DH1 = 128, 64, 2, 64
KEYS = VID * FR
KC = 512
VC = KC // FR
NKC = KEYS // KC
SUB = KC // P
SPARE = E * P
RW = D + 2
SLOT_TILES = {1: G + E, 2: 2 * G + E}
LN_EPS, RMS_EPS = 1e-5, 1e-6
BIG = 1e30


def shape_constants():
    p = np.arange(P)
    block = np.zeros((P, H0, V1))
    for h in range(H0):
        block[h * DH0:(h + 1) * DH0, h] = 1.0
    pos = np.arange(TB)[None, :] * P + p[:, None]
    inv = (1.0 / np.float32(10000.0) ** (np.arange(0, DH0, 2, dtype=np.float32) / DH0)).astype(np.float32)
    ang = pos[..., None].astype(np.float32) * inv
    e = np.arange(E)

    def row(v):
        return np.broadcast_to(np.asarray(v, np.float64).reshape(1, -1), (P, np.size(v)))

    cols = {
        "ident": np.eye(P),
        "causal": (p[None, :] >= p[:, None]) * 1.0,
        "before": (p[:, None] < p[None, :]) * 1.0,
        "headblock": block.reshape(P, -1),
        "cos": np.concatenate([np.cos(ang), np.cos(ang)], -1).reshape(P, -1),
        "sin": np.concatenate([-np.sin(ang), np.sin(ang)], -1).reshape(P, -1),
        "steps": pos + 1.0,
        "blockrow": np.stack([p * BLOCK, (p + P) * BLOCK], 1),
        "descend": row(E - e),
        "tiles128": row(np.arange(G) * P),
        "earlier": row((e[None, :] < e[:, None]) * 1.0),
        "minus_half": np.full((P, 1), -0.5),
        "token": np.arange(G)[None, :] * P + p[:, None],
        "slot": row(np.arange(SLOT_TILES[2])),
    }
    at, off = {}, 0
    for k, v in cols.items():
        at[k] = slice(off, off + v.shape[1])
        off += v.shape[1]
    return at, np.concatenate(list(cols.values()), 1).astype(np.float32)


AT, CONSTANTS = shape_constants()


class Steps:

    def __init__(self, engine, semaphore):
        self.engine, self.semaphore, self.base, self.k = engine, semaphore, 0, 0

    def mark(self, instruction):
        instruction.then_inc(self.semaphore, 1)
        self.k += 1

    def wait(self):
        self.engine.wait_ge(self.semaphore, self.base + self.k)

    def wait_apart(self, mark):
        self.wait()
        self.engine.memset(mark, 0.0)

    def then(self, instruction):
        self.mark(instruction)
        self.wait()

    def turn(self, i, per):
        self.outer, self.per = self.base + self.k, per
        self.base, self.k = self.outer + i * per, 0

    def end(self, turns):
        assert self.k == self.per, (self.k, self.per)
        self.base, self.k = self.outer + turns * self.per, 0


class Kept:

    def __init__(self, nc, ctx, has):
        def sb(n, s, d=F32):
            return ctx.enter_context(nc.sbuf_tensor(n, s, d))

        self.gathered = ctx.enter_context(nc.semaphore("gathered"))
        self.consts = sb("consts", [P, CONSTANTS.shape[1]])
        self.hidden = sb("hidden", [P, G, D])
        self.keys = sb("keys", [P, H1 * KEYS], F32R)
        self.values = sb("values", [P, H1, KEYS // P, DH1])
        self.wq2 = sb("wq2", [P, H1, P])
        self.wo2 = sb("wo2", [P, 2, D])
        self.bq2 = sb("bq2", [P, H1])
        self.bo_all = sb("bo_all", [P, D])
        self.neg_ident = sb("neg_ident", [P, P], F32R)
        self.rows_dram = nc.dram_tensor("chosen_rows", [N], U32).ap()
        self.routed_dram = {k: nc.dram_tensor(f"routed{k}", [t * P, RW], F32).ap() for k, t in SLOT_TILES.items()}
        self.result_dram = {k: nc.dram_tensor(f"result{k}", [SPARE + k * N, D], F32).ap() for k in SLOT_TILES}

    def const(self, name):
        return self.consts[:, AT[name]]


def inverse_root(pool, K, out, square):
    return pool.tensor_tensor(out, square, K.const("minus_half").to_broadcast([P, square.shape[1]]), ALU.pow)


def column(vector):
    return vector.rearrange("(p a) -> p a", a=1)


def everywhere(vector, width):
    return vector.rearrange("(a n) -> a n", a=1).to_broadcast([P, width])


def allocators(nc, ctx, phase):
    return (lambda n, s, d=F32: ctx.enter_context(nc.sbuf_tensor(f"{phase}_{n}", s, d)),
            lambda n, s, d=F32: ctx.enter_context(nc.psum_tensor(f"{phase}_{n}", s, d)),
            lambda n: ctx.enter_context(nc.semaphore(f"{phase}_{n}")))


def clear_semaphores(nc, first, last):
    with nc.Block() as block:
        @block.gpsimd
        def _(pool):
            pool.sem_clear(range(first.num, last.num + 1))


class LayerNorm:

    def __init__(self, nc, ctx, phase, scale=1.0, eps=LN_EPS):
        sb, _, sem = allocators(nc, ctx, phase)
        self.scale, self.eps = scale, eps
        self.rows = sb("rows", [P, 2, TB, D])
        self.stats, self.mv = sb("stats", [P, G, 6]), sb("mv", [P, G, 2])
        self.square, self.root = sb("square", [P, G]), sb("root", [P, G])
        self.steps, self.square_ready, self.root_ready = sem("norm_steps"), sem("square_ready"), sem("root_ready")

    def statistics(self, dve, hidden):
        with dve.Fori(0, B) as b:
            for i in range(TB):
                dve.bn_stats(self.stats[:, ds(b * TB + i, 1), :].rearrange("p a d -> p (a d)"),
                             hidden[:, ds(b * TB + i, 1), :].rearrange("p a d -> p (a d)")).then_inc(self.steps, 1)
        dve.wait_ge(self.steps, G)
        for g in range(G):
            dve.bn_aggr(self.mv[:, g, :], self.stats[:, g, :]).then_inc(self.steps, 1)
        dve.wait_ge(self.steps, 2 * G)
        dve.tensor_scalar(self.square[:], self.mv[:, :, 1], self.scale, self.eps, ALU.mult, ALU.add).then_inc(self.square_ready, 1)

    def roots(self, pool, K):
        pool.wait_ge(self.square_ready, 1)
        inverse_root(pool, K, self.root[:], self.square[:]).then_inc(self.root_ready, 1)

    def batch(self, dve, b, s, hidden, used, ready):
        dve.wait_ge(used, b + 1)
        for i in range(TB):
            g = ds(b * TB + i, 1)
            ins = dve.tensor_scalar(self.rows[:, s, i, :], hidden[:, g, :].rearrange("p a d -> p (a d)"),
                                    self.mv[:, g, 0], self.root[:, g], ALU.subtract, ALU.mult)
        ins.then_inc(ready, 1)


def select_and_project(nc, a, K):
    with ExitStack() as ctx:
        sb, ps, sem = allocators(nc, ctx, "select")
        CT = 8
        TURNS = BLOCK // CT // 4
        xbuf = sb("xbuf", [P, 4, 2, CT, D])
        prod = sb("prod", [P, 2, 2, CT, D])
        wtok = sb("wtok", [P, D])
        btok = sb("btok", [P, 1])
        scores = sb("scores", [P, 2, BLOCK])
        rest = sb("rest", [P, 2, BLOCK])
        best = sb("best", [P, 2, TOP])
        besti = sb("besti", [P, 2, TOP], U32)
        rows = sb("rows", [P, 2, TOP], U32)
        rowidx = sb("rowidx", [P, G], U32)
        wraw = sb("wraw", [P, 5, D])
        wk2 = sb("wk2", [P, H1, P])
        wvT = sb("wvT", [P, D])
        bk2 = sb("bk2", [P, H1])
        bv_all = sb("bv_all", [P, D])
        emb = sb("emb", [P, 4, SUB, D])
        embT = sb("embT", [P, 2, KC])
        psT = ps("psT", [P, 2, KC])
        psK = ps("psK", [P, H1, KC])
        psV = ps("psV", [P, 2, KC])
        consts_in, weights_in = sem("consts_in"), sem("weights_in")
        x_in = [sem(f"x_in{i}") for i in range(4)]
        emb_in = [sem(f"emb_in{i}") for i in range(4)]
        odd_products, chunks_reduced, select_steps = sem("odd_products"), sem("chunks_reduced"), sem("select_steps")
        weightT_ready, weightT_copied = sem("weightT_ready"), sem("weightT_copied")
        embT_ready, embT_copied = sem("embT_ready"), sem("embT_copied")
        keys_ready, values_ready = sem("keys_ready"), sem("values_ready")
        key_highs, key_lows, values_done = sem("key_highs"), sem("key_lows"), sem("values_done")
        rows_chosen, rows_out, rows_back = sem("rows_chosen"), sem("rows_out"), sem("rows_back")

        weights_landed = 16 * (7 + 4 * H1 + 2)

        x_chunks = a["x"].rearrange("b (k t) d -> (b k) (t d)", t=BLOCK).rearrange("(f p) n -> p f n", p=P)
        emb_rows = a["L1_attn_video_embeds"].rearrange("v f d -> (v f) d").rearrange("(t p) d -> p t d", p=P)
        ident = K.const("ident")
        per_token = [P, 2 * CT, D]

        with nc.Block() as block:
            @block.sync
            def _(sp):
                sp.dma_start(K.consts[:], a["shape_constants"]).then_inc(consts_in, 16)
                sp.dma_start(wtok[:], everywhere(a["L0_tok_W"].rearrange("a n -> (a n)"), D)).then_inc(consts_in, 16)
                sp.dma_start(btok[:], everywhere(a["L0_tok_b"], 1)).then_inc(consts_in, 16)

                def load(c, s):
                    sp.dma_start(xbuf[:, s, :, :, :].rearrange("p f t d -> p f (t d)"),
                                 x_chunks[:, :, ds(c * CT * D, CT * D)]).then_inc(x_in[s], 16)

                for s in range(4):
                    load(s, s)
                with sp.Fori(1, TURNS) as it:
                    for s in range(4):
                        sp.wait_ge(chunks_reduced, (it - 1) * 4 + s + 3)
                        load(it * 4 + s, s)
                sp.wait_ge(rows_chosen, 2)
                sp.dma_start(K.rows_dram.rearrange("(f p r) -> p f r", p=P, r=TOP), rows[:]).then_inc(rows_out, 16)
                sp.wait_ge(rows_out, 16)
                sp.dma_start(rowidx[:], K.rows_dram.rearrange("(g p) -> p g", p=P),
                             allow_slow_non_contiguous=True).then_inc(rows_back, 16)

            @block.gpsimd
            def _(pool):
                pool.wait_ge(consts_in, 48)
                with pool.Fori(0, TURNS) as it:
                    for s in (1, 3):
                        pool.wait_ge(x_in[s], (it + 1) * 16)
                        pool.wait_ge(chunks_reduced, it * 4 + s + 1)
                        pool.tensor_tensor(prod[:, 1].rearrange("p f t d -> p (f t) d"),
                                           xbuf[:, s].rearrange("p f t d -> p (f t) d"),
                                           wtok[:, None, :].to_broadcast(per_token), ALU.mult).then_inc(odd_products, 1)
                pool.wait_ge(rows_back, 16)
                for g in range(G):
                    pool.indirect_dma_start(K.hidden[:, g, :], None, a["x"].rearrange("b s d -> (b s) d"),
                                            bass.IndirectOffsetOnAxis(ap=rowidx[:, g:g + 1], axis=0)).then_inc(K.gathered, 16)
                pool.wait_ge(K.gathered, 16 * G)

            @block.vector
            def _(dve):
                steps = Steps(dve, select_steps)
                dve.nop().then_inc(chunks_reduced, 2)
                dve.nop().then_inc(key_lows, H1)
                dve.nop().then_inc(values_done, 2)
                dve.wait_ge(consts_in, 48)
                steps.mark(dve.tensor_scalar(K.neg_ident[:], ident, -1.0, None, ALU.mult))
                dve.wait_ge(weights_in, weights_landed)
                with dve.Fori(0, TURNS) as it:
                    steps.turn(it, 2)
                    for s in range(4):
                        c = it * 4 + s
                        if s % 2 == 0:
                            dve.wait_ge(x_in[s], (it + 1) * 16)
                            steps.then(dve.tensor_tensor(prod[:, 0].rearrange("p f t d -> p (f t) d"),
                                                         xbuf[:, s].rearrange("p f t d -> p (f t) d"),
                                                         wtok[:, None, :].to_broadcast(per_token), ALU.mult))
                        else:
                            dve.wait_ge(odd_products, it * 2 + s // 2 + 1)
                        dve.tensor_reduce(scores[:, :, ds(c * CT, CT)], prod[:, s % 2], X, ALU.add).then_inc(chunks_reduced, 1)
                        if s % 2 == 0:
                            dve.wait_ge(chunks_reduced, c + 3)
                        for h in range(H1):
                            dve.wait_ge(key_highs, c * H1 + h + 1)
                            cols = ds(c * KC + h * KEYS, KC)
                            dve.scalar_tensor_tensor(K.keys[64:P, cols], psK[64:P, h, :], bk2[64:P, h:h + 1],
                                                     K.keys[64:P, cols].bitcast(F32), ALU.add, ALU.subtract).then_inc(key_lows, 1)
                        dve.wait_ge(values_ready, c + 1)
                        dve.tensor_tensor(K.values[:, :, ds(c * SUB, SUB), :].rearrange("p h t e -> p t h e"),
                                          psV[:, s % 2, :].rearrange("p (t h e) -> p t h e", t=SUB, h=H1),
                                          bv_all[:].rearrange("p (h e) -> p h e", h=H1)[:, None].to_broadcast([P, SUB, H1, DH1]),
                                          ALU.add).then_inc(values_done, 1)
                steps.end(TURNS)
                dve.wait_ge(chunks_reduced, 4 * TURNS + 2)
                steps.then(dve.tensor_scalar(scores[:], scores[:], btok[:, 0:1], None, ALU.add))
                for f in range(2):
                    steps.then(dve.max(best[:, f, 0:8], scores[:, f, :]))
                    steps.mark(dve.max_index(besti[:, f, 0:8], best[:, f, 0:8], scores[:, f, :]))
                    steps.then(dve.match_replace(rest[:, f, :], best[:, f, 0:8], scores[:, f, :], -3e38))
                    steps.then(dve.max(best[:, f, 8:16], rest[:, f, :]))
                    steps.then(dve.max_index(besti[:, f, 8:16], best[:, f, 8:16], rest[:, f, :]))
                    dve.tensor_scalar(rows[:, f, :], besti[:, f, :], K.const("blockrow")[:, f:f + 1], None,
                                      ALU.add).then_inc(rows_chosen, 1)

            @block.scalar
            def _(act):
                for j, n in enumerate(("Wq", "Wk", "Wv")):
                    act.dma_start(wraw[:, j, :], a["L1_attn_" + n]).then_inc(weights_in, 16)
                for side in range(2):
                    for copy in range(2):
                        act.dma_start(wraw[:, 3 + side, copy * DH1:(copy + 1) * DH1],
                                      a["L1_attn_Wo"][:, side * DH1:(side + 1) * DH1]).then_inc(weights_in, 16)
                for h in range(H1):
                    for part in (slice(0, 64), slice(64, P)):
                        act.dma_start(bk2[part, h:h + 1], column(a["L1_attn_bk"][h * DH1:(h + 1) * DH1])).then_inc(weights_in, 16)
                        act.dma_start(K.bq2[part, h:h + 1], column(a["L1_attn_bq"][h * DH1:(h + 1) * DH1])).then_inc(weights_in, 16)
                act.dma_start(bv_all[:], everywhere(a["L1_attn_bv"], D)).then_inc(weights_in, 16)
                act.dma_start(K.bo_all[:], everywhere(a["L1_attn_bo"], D)).then_inc(weights_in, 16)

                def load(c, s):
                    act.dma_start(emb[:, s], emb_rows[:, ds(c * SUB, SUB), :]).then_inc(emb_in[s], 16)

                for s in range(4):
                    load(s, s)
                act.wait_ge(weightT_ready, 5)
                for h in range(H1):
                    for part in range(2):
                        half = slice(part * DH1, (part + 1) * DH1)
                        head = slice(h * DH1, (h + 1) * DH1)
                        act.activation(K.wq2[:, h, half], psT[:, 0, 0:D][:, head], ACT.Copy).then_inc(weightT_copied, 1)
                        act.activation(wk2[:, h, half], psT[:, 0, D:2 * D][:, head], ACT.Copy).then_inc(weightT_copied, 1)
                act.activation(wvT[:], psT[:, 0, 2 * D:3 * D], ACT.Copy).then_inc(weightT_copied, 1)
                for side in range(2):
                    act.activation(K.wo2[:, side, :], psT[:, side, 3 * D:4 * D], ACT.Copy).then_inc(weightT_copied, 1)

                def chunk(c, s, ahead):
                    act.wait_ge(embT_ready, c + 1)
                    act.activation(embT[:, s % 2, :], psT[:, s % 2, :], ACT.Copy).then_inc(embT_copied, 1)
                    if ahead:
                        load(c + 4, s)
                    for h in range(H1):
                        act.wait_ge(keys_ready, c * H1 + h + 1)
                        act.activation(K.keys[:, ds(c * KC + h * KEYS, KC)], psK[:, h, :], ACT.Identity,
                                       bias=bk2[:, h:h + 1]).then_inc(key_highs, 1)

                with act.Fori(0, TURNS - 1) as it:
                    for s in range(4):
                        chunk(it * 4 + s, s, True)
                for s in range(4):
                    chunk((TURNS - 1) * 4 + s, s, False)

            @block.tensor
            def _(pe):
                pe.wait_ge(consts_in, 48)
                pe.wait_ge(weights_in, weights_landed)
                for j in range(5):
                    at = min(j, 3) * D
                    pe.transpose(psT[:, j // 4, at:at + D], wraw[:, j, :], ident).then_inc(weightT_ready, 1)
                pe.wait_ge(weightT_copied, 4 * H1 + 3)
                with pe.Fori(0, TURNS) as it:
                    for s in range(4):
                        c = it * 4 + s
                        pe.wait_ge(emb_in[s], (it + 1) * 16)
                        for t in range(SUB):
                            mm = pe.transpose(psT[:, s % 2, t * P:(t + 1) * P], emb[:, s, t, :], ident)
                        mm.then_inc(embT_ready, 1)
                        pe.wait_ge(embT_copied, c + 1)
                        pe.wait_ge(key_lows, (c + 1) * H1)
                        for h in range(H1):
                            pe.matmul(psK[:, h, :], wk2[:, h, :], embT[:, s % 2, :], start=True, stop=True).then_inc(keys_ready, 1)
                        pe.wait_ge(values_done, c + 1)
                        for t in range(SUB):
                            mm = pe.matmul(psV[:, s % 2, t * P:(t + 1) * P], embT[:, s % 2, t * P:(t + 1) * P], wvT[:],
                                           start=True, stop=True, skip_group_check=True)
                        mm.then_inc(values_ready, 1)

        clear_semaphores(nc, consts_in, rows_back)


def zero_dram(sp, K, zeros, done):
    for k, tiles in SLOT_TILES.items():
        view = K.routed_dram[k].rearrange("(n p) d -> p n d", p=P)
        for j in range(0, tiles, E):
            sp.dma_start(view[:, j:j + E, :], zeros[:]).then_inc(done, 16)


def retention(nc, a, K):
    with ExitStack() as ctx:
        sb, _, sem = allocators(nc, ctx, "retention")
        qkv = sb("qkv", [P, G, 2 * D + H0 * V1])
        gate_out = sb("gate_out", [P, G, D])
        params = sb("params", [P, G, H0, 4])
        gate = sb("gate", [P, G, H0])
        decay = sb("decay", [P, TB, H0])
        kscale = sb("kscale", [P, TB, H0])
        rope_c = sb("rope_c", [P, TB, 2, DH0])
        rope_s = sb("rope_s", [P, TB, 2, DH0])
        wp = sb("wp", [P, D])
        s_const, s_latent, s_gates = sem("ret_weights_in"), sem("latent_ready"), sem("gate_steps")
        xn_ready, xnT_ready, xnT_copied = sem("xn_ready"), sem("xnT_ready"), sem("xnT_copied")
        latent_done, qkv_ready, qkv_copied = sem("latent_done"), sem("qkv_ready"), sem("qkv_copied")
        gate_ready, gate_done = sem("gate_ready"), sem("gate_done")
        ident = K.const("ident")

        with ExitStack() as inner:
            sb1, ps1, _ = allocators(nc, inner, "project")
            zeros = sb1("zeros", [P, E, RW])
            wc = sb1("wc", [P, LAT])
            wall = sb1("wall", [LAT, QKV + D])
            lnw, memw = sb1("lnw", [P, 1]), sb1("memw", [P, 1])
            qkw = sb1("qkw", [P, 2, DH0])
            temp, hd = sb1("temp", [P, 1]), sb1("hd", [P, H0])
            norm = LayerNorm(nc, inner, "projectnorm", 1.0 + RMS_EPS, LN_EPS * RMS_EPS)
            xnT = sb1("xnT", [P, L])
            latT = sb1("latT", [LAT, 2, L])
            sg = params
            dph, amp = sb1("dph", [P, G, H0]), sb1("amp", [P, G, H0])
            rate = sb1("rate", [P, 4, H0])
            cld = sb1("cld", [P, TB, H0])
            half_pi = sb1("half_pi", [P, 1])
            psT = ps1("psT", [P, L])
            psL = ps1("psL", [LAT, L])
            psQ = ps1("psQ", [P, 2, 512])
            psG = ps1("psG", [P, 2, TB, D])
            zeroed, zeros_set = sem("routed_zeroed"), sem("zeros_set")
            weights_ready, act_gates = sem("ret_weights_ready"), sem("act_gates")

            with nc.Block() as block:
                @block.sync
                def _(sp):
                    sp.dma_start(wc[:], a["L0_attn_Wc"]).then_inc(s_const, 16)
                    sp.dma_start(wall[:, 0:3 * D], a["L0_attn_Wqkv"]).then_inc(s_const, 16)
                    sp.dma_start(wall[:, 3 * D:QKV], a["L0_attn_Wreso"]).then_inc(s_const, 16)
                    sp.dma_start(wall[:, QKV:QKV + D], a["L0_attn_Wg"]).then_inc(s_const, 16)
                    sp.dma_start(wp[:], a["L0_attn_Wp"]).then_inc(s_const, 16)
                    sp.dma_start(lnw[:], column(a["L0_attn_ln_w"])).then_inc(s_const, 16)
                    sp.dma_start(memw[:], column(a["L0_attn_mem_w"])).then_inc(s_const, 16)
                    sp.dma_start(qkw[:, 0, :], everywhere(a["L0_attn_qn_w"], DH0)).then_inc(s_const, 16)
                    sp.dma_start(qkw[:, 1, :], everywhere(a["L0_attn_kn_w"], DH0)).then_inc(s_const, 16)
                    sp.dma_start(temp[:], everywhere(a["L0_attn_temperature"], 1)).then_inc(s_const, 16)
                    sp.dma_start(hd[:], everywhere(a["L0_attn_head_decay"], H0)).then_inc(s_const, 16)
                    sp.wait_ge(zeros_set, 2)
                    zero_dram(sp, K, zeros, zeroed)
                    sp.wait_ge(zeroed, 16 * sum(SLOT_TILES.values()) // E)

                @block.gpsimd
                def _(pool):
                    pool.memset(zeros[:], 0.0).then_inc(zeros_set, 1)
                    norm.roots(pool, K)

                @block.vector
                def _(dve):
                    dve.wait_ge(zeros_set, 1)
                    dve.tensor_copy(zeros[:, :, D].bitcast(U32), K.const("token")[:, 0:E]).then_inc(zeros_set, 1)
                    norm.statistics(dve, K.hidden)
                    dve.wait_ge(s_const, 16 * 11)
                    dve.tensor_scalar(wc[:], wc[:], lnw[:, 0:1], None, ALU.mult).then_inc(weights_ready, 1)
                    dve.tensor_scalar(wp[:], wp[:], memw[:, 0:1], None, ALU.mult).then_inc(weights_ready, 1)
                    dve.wait_ge(norm.root_ready, 1)
                    with dve.Fori(0, B // 2) as it:
                        for s in range(2):
                            norm.batch(dve, it * 2 + s, s, K.hidden, xnT_copied, xn_ready)
                    steps = Steps(dve, s_gates)
                    for j in range(2):
                        w = qkw[:, j, :]
                        cos = K.const("cos").rearrange("p (i d) -> p i d", i=TB)
                        sin = K.const("sin").rearrange("p (i d) -> p i d", i=TB)
                        hw = DH0 // 2
                        steps.mark(dve.tensor_tensor(rope_c[:, :, j, :], cos, w[:, None, :].to_broadcast([P, TB, DH0]), ALU.mult))
                        steps.mark(dve.tensor_tensor(rope_s[:, :, j, 0:hw], sin[:, :, 0:hw], w[:, None, hw:DH0].to_broadcast([P, TB, hw]), ALU.mult))
                        steps.mark(dve.tensor_tensor(rope_s[:, :, j, hw:DH0], sin[:, :, hw:DH0], w[:, None, 0:hw].to_broadcast([P, TB, hw]), ALU.mult))
                    steps.mark(dve.memset(half_pi[:], float(np.pi / 2)))
                    dve.wait_ge(act_gates, 1)
                    steps.then(dve.tensor_tensor(dph[:], sg[:, :, :, 1], sg[:, :, :, 3], ALU.subtract))
                    steps.then(dve.scalar_tensor_tensor(dph[:], dph[:], -1.0, dph[:], ALU.mult, ALU.max))
                    steps.then(dve.tensor_tensor(amp[:], sg[:, :, :, 0], sg[:, :, :, 2], ALU.mult))
                    dve.wait_ge(act_gates, 3)
                    steps.then(dve.tensor_tensor(amp[:], amp[:], gate[:], ALU.mult))
                    steps.then(dve.tensor_scalar(amp[:], amp[:], temp[:, 0:1], None, ALU.mult))
                    steps.then(dve.tensor_scalar(rate[:, 1, :], rate[:, 0, :], 0.65, 0.3, ALU.mult, ALU.add))
                    steps.then(dve.tensor_scalar(rate[:, 2, :], rate[:, 1, :], 1e-5, 0.999, ALU.max, ALU.min))
                    steps.then(dve.tensor_scalar(rate[:, 3, :], rate[:, 2, :], -1.0, 1.0, ALU.mult, ALU.add))
                    dve.wait_ge(act_gates, 5)
                    steps.then(dve.tensor_tensor(cld[:], K.const("steps")[:, :, None].to_broadcast([P, TB, H0]),
                                                 rate[:, 0:1, :].to_broadcast([P, TB, H0]), ALU.mult))
                    steps.then(dve.tensor_scalar(gate[:], gate[:], 1.2, -0.1, ALU.mult, ALU.add))
                    steps.then(dve.tensor_scalar(gate[:], gate[:], 0.05, 0.95, ALU.max, ALU.min))
                    dve.wait_ge(act_gates, 6)
                    steps.then(dve.tensor_scalar(kscale[:], decay[:], 1e-8, None, ALU.add))
                    steps.then(dve.reciprocal(kscale[:], kscale[:]))
                    steps.then(dve.tensor_tensor(kscale[:], kscale[:], rate[:, 3:4, :].to_broadcast([P, TB, H0]), ALU.mult))

                @block.scalar
                def _(act):
                    act.nop().then_inc(xnT_copied, 2)
                    act.nop().then_inc(latent_done, 1)
                    act.nop().then_inc(qkv_copied, 2)
                    act.nop().then_inc(gate_done, 2)

                    def turned(b):
                        act.wait_ge(xnT_ready, b + 1)
                        act.activation(xnT[:], psT[:], ACT.Copy).then_inc(xnT_copied, 1)

                    def latent(b, s):
                        act.wait_ge(s_latent, b + 1)
                        act.activation(latT[:, s, :], psL[:], ACT.Silu).then_inc(latent_done, 1)

                    def keep(b, i):
                        g = b * TB + i
                        act.wait_ge(qkv_ready, g + 1)
                        row = qkv[:, ds(g, 1), :].rearrange("p a d -> p (a d)")
                        act.activation(row[:, 0:2 * D], psQ[:, i % 2, 0:2 * D], ACT.Copy)
                        act.activation(row[:, 2 * D:].rearrange("p (h e) -> p h e", h=H0)[:, :, 0:DH0],
                                       psQ[:, i % 2, 2 * D:3 * D].rearrange("p (h e) -> p h e", h=H0), ACT.Copy)
                        act.activation(params[:, ds(g, 1)].rearrange("p a h c -> p (a h c)"), psQ[:, i % 2, 3 * D:QKV], ACT.Copy).then_inc(qkv_copied, 1)

                    def batch(b, s, more=True):
                        if more:
                            turned(b + 1)
                        keep(b, 0)
                        keep(b, 1)
                        if more:
                            latent(b + 1, 1 - s)
                        keep(b, 2)
                        keep(b, 3)
                        act.wait_ge(gate_ready, b + 1)
                        act.activation(gate_out[:, ds(b * TB, TB), :], psG[:, s], ACT.Silu).then_inc(gate_done, 1)

                    turned(0)
                    latent(0, 0)
                    with act.Fori(0, B // 2 - 1) as it:
                        for s in range(2):
                            batch(it * 2 + s, s)
                    batch(B - 2, 0)
                    batch(B - 1, 1, False)
                    act.wait_ge(qkv_copied, G + 2)
                    act.activation(sg[:], params[:], ACT.Sigmoid).then_inc(act_gates, 1)
                    act.activation(rate[:, 0, :], hd[:], ACT.Sigmoid).then_inc(act_gates, 1)
                    act.wait_ge(s_gates, 9)
                    act.activation(gate[:], dph[:], ACT.Sin, bias=half_pi[:, 0:1], scale=-float(np.pi)).then_inc(act_gates, 1)
                    act.wait_ge(s_gates, 12)
                    act.activation(gate[:], amp[:], ACT.Sigmoid).then_inc(act_gates, 1)
                    act.wait_ge(s_gates, 14)
                    act.activation(rate[:, 0, :], rate[:, 2, :], ACT.Ln).then_inc(act_gates, 1)
                    act.wait_ge(s_gates, 16)
                    act.activation(decay[:], cld[:], ACT.Exp).then_inc(act_gates, 1)

                @block.tensor
                def _(pe):
                    pe.wait_ge(weights_ready, 2)

                    def turn_rows(b, s):
                        pe.wait_ge(xn_ready, b + 1)
                        pe.wait_ge(xnT_copied, b + 2)
                        for i in range(TB):
                            mm = pe.transpose(psT[:, i * P:(i + 1) * P], norm.rows[:, s, i, :], ident)
                        mm.then_inc(xnT_ready, 1)

                    def latent(b):
                        pe.wait_ge(xnT_copied, b + 3)
                        pe.wait_ge(latent_done, b + 1)
                        pe.matmul(psL[:], wc[:], xnT[:], start=True, stop=True).then_inc(s_latent, 1)

                    def project(b, s, i):
                        if i == 0:
                            pe.wait_ge(latent_done, b + 2)
                            pe.wait_ge(gate_done, b + 1)
                        lat = latT[:, s, i * P:(i + 1) * P]
                        pe.wait_ge(qkv_copied, b * TB + i + 1)
                        pe.matmul(psQ[:, i % 2, 0:QKV], lat, wall[:, 0:QKV], start=True, stop=True).then_inc(qkv_ready, 1)
                        mm = pe.matmul(psG[:, s, i, :], lat, wall[:, QKV:QKV + D], start=True, stop=True, skip_group_check=True)
                        if i == TB - 1:
                            mm.then_inc(gate_ready, 1)

                    def batch(b, s, more=True):
                        if more:
                            turn_rows(b + 1, 1 - s)
                        project(b, s, 0)
                        project(b, s, 1)
                        if more:
                            latent(b + 1)
                        project(b, s, 2)
                        project(b, s, 3)

                    turn_rows(0, 0)
                    latent(0)
                    with pe.Fori(0, B // 2 - 1) as it:
                        for s in range(2):
                            batch(it * 2 + s, s)
                    batch(B - 2, 0)
                    batch(B - 1, 1, False)

        with ExitStack() as inner:
            sbf, _, _ = allocators(nc, inner, "features")
            t1, t2 = sbf("t1", [P, 2, TB, 2 * D]), sbf("t2", [P, 2, TB, 2 * D])
            square = sbf("square", [P, 2, 2, TB * 2 * H0])
            root = sbf("root", [P, 2, TB * 2 * H0])
            feature_steps, squared, exped, scaled, turned, lowered = (sem(n) for n in (
                "feature_steps", "squared", "exped", "qk_scaled", "rotated", "lowered"))
            qk_square_ready, qk_root_ready, features_ready = sem("qk_square_ready"), sem("qk_root_ready"), sem("features_ready")

            def queries_keys(b):
                return qkv[:, ds(b * TB, TB), 0:2 * D]


            with nc.Block() as block:
                @block.scalar
                def _(act):
                    def step(n, s, begins=True, ends=True):
                        if begins:
                            if ends:
                                act.wait_ge(features_ready, n)
                            act.activation(t1[:, s], queries_keys(n), ACT.Square).then_inc(squared, 1)
                        if ends:
                            act.wait_ge(lowered, n)
                            act.activation(t1[:, 1 - s], t1[:, 1 - s], ACT.Exp).then_inc(exped, 1)

                    step(0, 0, ends=False)
                    with act.Fori(0, B // 2 - 1) as it:
                        step(it * 2 + 1, 1)
                        step(it * 2 + 2, 0)
                    step(B - 1, 1)
                    step(B, 0, begins=False)

                @block.gpsimd
                def _(pool):
                    def rotate(b, s):
                        pool.wait_ge(qk_square_ready, b + 1)
                        inverse_root(pool, K, root[:, s], square[:, s, 1]).then_inc(qk_root_ready, 1)
                        pool.wait_ge(scaled, b + 1)
                        qk = queries_keys(b)
                        hw = DH0 // 2
                        for j in range(2):
                            part = slice(j * D, (j + 1) * D)
                            x = qk[:, :, part].rearrange("p i (h d) -> p i h d", h=H0)
                            sn = rope_s[:, :, j, :]
                            r2 = t2[:, s, :, part].rearrange("p i (h d) -> p i h d", h=H0)
                            pool.tensor_tensor(r2[:, :, :, 0:hw], x[:, :, :, hw:DH0], sn[:, :, None, 0:hw].to_broadcast([P, TB, H0, hw]), ALU.mult).then_inc(turned, 1)
                            pool.tensor_tensor(r2[:, :, :, hw:DH0], x[:, :, :, 0:hw], sn[:, :, None, hw:DH0].to_broadcast([P, TB, H0, hw]), ALU.mult).then_inc(turned, 1)

                    with pool.Fori(0, B // 2) as it:
                        for s in range(2):
                            rotate(it * 2 + s, s)

                @block.vector
                def _(dve):
                    steps = Steps(dve, feature_steps)
                    steps.mark(dve.memset(qkv[:, :, 2 * D:].rearrange("p g (h e) -> p g h e", h=H0)[:, :, :, DH0], 1.0))
                    dve.nop().then_inc(features_ready, 1)

                    def step(n, s, begins=True, ends=True):
                        o = 1 - s
                        if begins:
                            dve.wait_ge(squared, n + 1)
                            steps.then(dve.tensor_reduce(square[:, s, 0, :], t1[:, s].rearrange("p i (g d) -> p (i g) d", d=DH0), X, ALU.add))
                            dve.tensor_scalar(square[:, s, 1, :], square[:, s, 0, :], 1.0 / DH0, RMS_EPS, ALU.mult, ALU.add).then_inc(qk_square_ready, 1)
                        if ends:
                            dve.wait_ge(turned, n * 4)
                            steps.then(dve.tensor_tensor(t2[:, o], t1[:, o], t2[:, o], ALU.add))
                            dve.tensor_scalar(t1[:, o], t2[:, o], 0.0, None, ALU.min).then_inc(lowered, 1)
                        if begins:
                            dve.wait_ge(qk_root_ready, n + 1)
                            heads = queries_keys(n).rearrange("p i (g d) -> p i g d", d=DH0)
                            dve.tensor_tensor(heads, heads, root[:, s].rearrange("p (i g) -> p i g", i=TB)[:, :, :, None].to_broadcast([P, TB, 2 * H0, DH0]),
                                              ALU.mult).then_inc(scaled, 1)
                            dve.wait_ge(scaled, n + 1)
                            for j in range(2):
                                part = slice(j * D, (j + 1) * D)
                                steps.mark(dve.tensor_tensor(t1[:, s, :, part].rearrange("p i (h d) -> p i h d", h=H0),
                                                             queries_keys(n)[:, :, part].rearrange("p i (h d) -> p i h d", h=H0),
                                                             rope_c[:, :, j, None, :].to_broadcast([P, TB, H0, DH0]), ALU.mult))
                        if ends:
                            dve.wait_ge(exped, n)
                            steps.then(dve.scalar_tensor_tensor(t1[:, o], t2[:, o], 0.0, t1[:, o], ALU.max, ALU.add))
                            for j, scale in enumerate((decay, kscale)):
                                part = slice(j * D, (j + 1) * D)
                                dve.tensor_tensor(queries_keys(n - 1)[:, :, part].rearrange("p i (h d) -> p i h d", h=H0),
                                                  t1[:, o, :, part].rearrange("p i (h d) -> p i h d", h=H0),
                                                  scale[:, :, :, None].to_broadcast([P, TB, H0, DH0]), ALU.mult)
                            tiles = ds((n - 1) * TB, TB)
                            values = qkv[:, tiles, 2 * D:].rearrange("p i (h e) -> p i h e", h=H0)[:, :, :, 0:DH0]
                            dve.tensor_tensor(values, values, gate[:, tiles, :][:, :, :, None].to_broadcast([P, TB, H0, DH0]),
                                              ALU.mult).then_inc(features_ready, 1)

                    step(0, 0, ends=False)
                    with dve.Fori(0, B // 2 - 1) as it:
                        steps.turn(it, 10)
                        step(it * 2 + 1, 1)
                        step(it * 2 + 2, 0)
                    steps.end(B // 2 - 1)
                    step(B - 1, 1)
                    step(B, 0, begins=False)

        with ExitStack() as inner:
            sb2, ps2, _ = allocators(nc, inner, "decayed")
            stage = sb2("stage", [P, 2, 2 * D])
            qkT = sb2("qkT", [P, 2, 2 * P])
            qdiag = sb2("qdiag", [P, 2, H0, P])
            probs = sb2("probs", [P, 2, H0, P])
            state = sb2("state", [P, 4, H0 * V1])
            den = sb2("den", [P, 2, H0])
            o = sb2("o", [P, 2, D])
            osq = sb2("osq", [P, D])
            oms = sb2("oms", [P, 2, 2])
            oroot = sb2("oroot", [P, 2])
            oT = sb2("oT", [P, 2, P])
            y = sb2("y", [P, 2, D])
            psQK, psS = ps2("psQK", [P, 2, 512]), ps2("psS", [P, 2, H0, P])
            psA, psW, psO, psY = ps2("psA", [P, 512]), ps2("psW", [P, 512]), ps2("psO", [P, 512]), ps2("psY", [P, 512])
            zero_set, staged, qkT_ready, qdiag_set = sem("qdiag_zeroed"), sem("staged"), sem("qkT_ready"), sem("qdiag_set")
            scores_ready, probs_ready, state_ready, state_masked = sem("scores_ready"), sem("probs_ready"), sem("state_ready"), sem("state_masked")
            acc_ready, acc_used, o_ready, o_root_ready, o_steps, oT_ready, oT_copied, y_ready, y_read, y_added = (sem(n) for n in (
                "acc_ready", "acc_used", "o_ready", "o_root_ready", "o_steps", "oT_ready", "oT_copied", "y_ready", "y_read", "y_added"))
            PT = 2 * TB
            STAGES = 6

            def turns(engine, *stages):
                with engine.Fori(0, B // 2) as it:
                    for k in range(PT + STAGES - 1):
                        for stage_of, lag in stages:
                            if 0 <= k - lag < PT:
                                n = k - lag
                                stage_of(it * PT + n, n, (it * 2 + n // TB) * (TB - 1) + n % TB)

            with nc.Block() as block:
                @block.gpsimd
                def _(pool):
                    pool.memset(qdiag[:], 0.0).then_inc(zero_set, 1)

                    def root_of(g, n, m):
                        pool.wait_ge(o_ready, g + 1)
                        pool.wait_ge(y_added, g + 1)
                        inverse_root(pool, K, oroot[:, n % 2:n % 2 + 1], oms[:, n % 2, 1:2]).then_inc(o_root_ready, 1)

                    turns(pool, (root_of, 3))

                @block.scalar
                def _(act):
                    act.nop().then_inc(qdiag_set, 2)
                    act.nop().then_inc(oT_copied, 1)
                    act.wait_ge(zero_set, 1)

                    def stage_tile(g, n, m):
                        act.wait_ge(qkT_ready, g + 1)
                        act.activation(stage[:, n % 2, :], qkv[:, ds(g, 1), 0:2 * D].rearrange("p a d -> p (a d)"), ACT.Copy).then_inc(staged, 1)

                    def spread(g, n, m):
                        act.wait_ge(qkT_ready, g + 3)
                        act.wait_ge(acc_ready, g + 1)
                        act.activation(qkT[:, n % 2, :], psQK[:, n % 2, 0:2 * P], ACT.Copy)
                        for h in range(H0):
                            r = slice(h * DH0, (h + 1) * DH0)
                            ins = act.activation(qdiag[r, n % 2, h, :], psQK[r, n % 2, 0:P], ACT.Copy)
                        ins.then_inc(qdiag_set, 1)

                    def copy_o(g, n, m):
                        act.wait_ge(oT_ready, g + 3)
                        act.wait_ge(y_ready, g + 1)
                        act.activation(oT[:, n % 2, :], psO[:, 0:P], ACT.Copy).then_inc(oT_copied, 1)

                    turns(act, (stage_tile, 0), (spread, 1), (copy_o, 4))

                @block.vector
                def _(dve):
                    dve.nop().then_inc(probs_ready, 2)
                    dve.nop().then_inc(state_masked, 1)
                    dve.nop().then_inc(acc_used, 1)
                    dve.nop().then_inc(y_read, 1)
                    dve.nop().then_inc(y_added, 2)

                    def mask(g, n, m):
                        dve.wait_ge(acc_ready, g + 1)
                        dve.wait_ge(scores_ready, g + 1)
                        dve.tensor_tensor(probs[:, n % 2], psS[:, n % 2], K.const("causal")[:, None, :].to_broadcast([P, H0, P]),
                                          ALU.mult).then_inc(probs_ready, 1)

                    def keep_state(g, n, m):
                        if n % TB == TB - 1:
                            return
                        dve.wait_ge(state_ready, m + 1)
                        dve.tensor_tensor(state[:, n % 4, :], psW[:, 0:H0 * V1], K.const("headblock"), ALU.mult).then_inc(state_masked, 1)

                    def divide(g, n, m):
                        dve.wait_ge(acc_ready, g + 3)
                        dve.wait_ge(oT_ready, g + 1)
                        acc = psA[:, 0:H0 * V1].rearrange("p (h e) -> p h e", h=H0)
                        out = o[:, n % 2, :]
                        dve.tensor_scalar(den[:, 0, :], acc[:, :, DH0], 1e-5, None, ALU.max).then_inc(o_steps, 1)
                        dve.wait_ge(o_steps, g * 3 + 1)
                        dve.reciprocal(den[:, 1, :], den[:, 0, :]).then_inc(o_steps, 1)
                        dve.wait_ge(o_steps, g * 3 + 2)
                        dve.tensor_tensor(out.rearrange("p (h d) -> p h d", h=H0), acc[:, :, 0:DH0],
                                          den[:, 1, :, None].to_broadcast([P, H0, DH0]), ALU.mult).then_inc(acc_used, 1)
                        dve.wait_ge(acc_used, g + 2)
                        dve.tensor_tensor_reduce(osq[:], out, out, 1.0, 0.0, ALU.mult, ALU.add, oms[:, n % 2, 0:1]).then_inc(o_steps, 1)
                        dve.wait_ge(o_steps, g * 3 + 3)
                        dve.tensor_scalar(oms[:, n % 2, 1:2], oms[:, n % 2, 0:1], 1.0 / D, RMS_EPS, ALU.mult, ALU.add).then_inc(o_ready, 1)

                    def finish(g, n, m):
                        dve.wait_ge(o_root_ready, g + 1)
                        dve.wait_ge(y_ready, g + 3)
                        dve.wait_ge(y_added, g + 1)
                        dve.scalar_tensor_tensor(y[:, n % 2, :], psY[:, 0:D], oroot[:, n % 2:n % 2 + 1], gate_out[:, ds(g, 1), :].rearrange("p a d -> p (a d)"),
                                                 ALU.mult, ALU.mult).then_inc(y_read, 1)
                        dve.wait_ge(y_read, g + 2)
                        row = K.hidden[:, ds(g, 1), :].rearrange("p a d -> p (a d)")
                        dve.tensor_tensor(row, row, y[:, n % 2, :], ALU.add).then_inc(y_added, 1)

                    turns(dve, (mask, 2), (keep_state, 1), (finish, 5), (divide, 3))

                @block.tensor
                def _(pe):
                    pe.nop().then_inc(qkT_ready, 2)
                    pe.nop().then_inc(acc_ready, 2)
                    pe.nop().then_inc(oT_ready, 2)
                    pe.nop().then_inc(y_ready, 2)

                    def values_of(g):
                        return qkv[:, ds(g, 1), 2 * D:].rearrange("p a d -> p (a d)")

                    def turn_tile(g, n, m):
                        pe.wait_ge(staged, g + 1)
                        if n % TB < TB - 1:
                            pe.wait_ge(state_masked, m + 1)
                            pe.matmul(psW[:, 0:H0 * V1], stage[:, n % 2, D:2 * D], values_of(g), start=(n % TB == 0), stop=True,
                                      skip_group_check=True).then_inc(state_ready, 1)
                        pe.wait_ge(qdiag_set, g + 1)
                        pe.transpose(psQK[:, n % 2, 0:P], stage[:, n % 2, 0:D], ident)
                        pe.transpose(psQK[:, n % 2, P:2 * P], stage[:, n % 2, D:2 * D], ident).then_inc(qkT_ready, 1)

                    def score(g, n, m):
                        pe.wait_ge(qdiag_set, g + 3)
                        pe.wait_ge(probs_ready, g + 1)
                        pe.matmul(psS[:, n % 2].rearrange("p h l -> p (h l)"), qkT[:, n % 2, P:2 * P], qdiag[:, n % 2].rearrange("p h l -> p (h l)"),
                                  start=True, stop=True).then_inc(scores_ready, 1)

                    def add_up(g, n, m):
                        pe.wait_ge(acc_used, g + 1)
                        first = n % TB == 0
                        if not first:
                            pe.wait_ge(state_masked, m + 1)
                            pe.matmul(psA[:, 0:H0 * V1], qkT[:, n % 2, 0:P], state[:, (n - 1) % 4, :], start=True, stop=False, skip_group_check=True)
                        pe.wait_ge(probs_ready, g + 3)
                        for h in range(H0):
                            mm = pe.matmul(psA[:, h * V1:(h + 1) * V1], probs[:, n % 2, h, :], values_of(g)[:, h * V1:(h + 1) * V1],
                                           start=(first and h == 0), stop=True, skip_group_check=True)
                        mm.then_inc(acc_ready, 1)

                    def turn_o(g, n, m):
                        pe.wait_ge(o_ready, g + 1)
                        pe.wait_ge(oT_copied, g + 1)
                        pe.transpose(psO[:, 0:P], o[:, n % 2, :], ident).then_inc(oT_ready, 1)

                    def project(g, n, m):
                        pe.wait_ge(oT_copied, g + 2)
                        pe.wait_ge(y_read, g + 1)
                        pe.matmul(psY[:, 0:D], oT[:, n % 2, :], wp[:], start=True, stop=True).then_inc(y_ready, 1)

                    turns(pe, (score, 2), (turn_tile, 1), (project, 5), (turn_o, 4), (add_up, 3))

        clear_semaphores(nc, s_const, y_added)


def route_and_mix(nc, a, K, top, out=None):
    last = top == 2
    if last:
        names = {"router": "L1_ffn_router_w", "w1": "L1_ffn_w1", "b1": "L1_ffn_b1", "w2": "L1_ffn_w2", "b2": "L1_ffn_b2"}
    else:
        names = {"router": "L0_ffn_Wr", "w1": "L0_ffn_W1", "b1": "L0_ffn_b1", "w2": "L0_ffn_W2", "b2": "L0_ffn_b2"}
    tiles = SLOT_TILES[top]
    phase = f"moe{top}"
    with ExitStack() as ctx:
        sb, ps, sem = allocators(nc, ctx, phase)
        ident = K.const("ident")
        w1 = sb("w1", [P, E, F])
        w2 = sb("w2", [P, E, FC, D])
        b1 = sb("b1", [P, FC, E])
        b2 = sb("b2", [P, E, D])
        slots = sb("slots", [P, top, G], U32)
        share = sb("share", [P, 2, G])
        owner = sb("owner", [1, tiles], I32)
        if last:
            gamma, beta = sb("gamma", [P, E, D]), sb("beta", [P, E, D])
        router_in, weights_in, bias_set = sem("router_in"), sem("weights_in"), sem("bias_set")
        weights_landed = 16 * ((2 if last else 0) + 3 + FC)

        with ExitStack() as inner:
            sbr, psr, _ = allocators(nc, inner, phase + "route")
            norm = LayerNorm(nc, inner, phase + "norm")
            normed = sbr("normed", [P, G, RW])
            router = sbr("router", [P, E])
            router_bias = sbr("router_bias", [P, E])
            normT = sbr("normT", [P, 2, L])
            logits = sbr("logits", [P, G, E])
            picked = [sbr(f"picked{k}", [P, G, E]) for k in range(top)]
            work, equal = sbr("work", [P, G, E]), sbr("equal", [P, G, E])
            peak = sbr("peak", [P, 2, G])
            picks = sbr("picks", [P, G, E], BF16)
            before, all_ones = sbr("before", [P, P], BF16), sbr("all_ones", [P, P], BF16)
            many = sbr("many", [P, E, G])
            count, first, end = sbr("count", [P, E]), sbr("first", [P, E]), sbr("end", [P, E])
            pairs = sbr("pairs", [P, E, E])
            place = sbr("place", [P, G])
            passed = sbr("passed", [1, tiles, E])
            tile_expert = sbr("tile_expert", [1, tiles])
            psT = psr("psT", [P, 2, L])
            psR = psr("psR", [P, 512])
            psC, psN = psr("psC", [P, 512]), psr("psN", [P, 512])
            peaks_apart = sem("peaks_apart")
            norm_ready, normT_ready, normT_copied, rows_kept = sem("norm_ready"), sem("normT_ready"), sem("normT_copied"), sem("rows_kept")
            logits_ready, route_steps = sem("logits_ready"), sem("route_steps")
            picks_ready, ranks_ready, gates_exped, slots_ready, tagged, routed = (sem(n) for n in (
                "picks_ready", "ranks_ready", "gates_exped", "slots_ready", "tagged", "routed"))

            with nc.Block() as block:
                @block.sync
                def _(sp):
                    sp.dma_start(router[:], a[names["router"]]).then_inc(router_in, 16)
                    if last:
                        sp.dma_start(gamma[:].rearrange("p e d -> p (e d)"), everywhere(a["L1_ffn_gamma"].rearrange("e d -> (e d)"), E * D)).then_inc(weights_in, 16)
                        sp.dma_start(beta[:].rearrange("p e d -> p (e d)"), everywhere(a["L1_ffn_beta"].rearrange("e d -> (e d)"), E * D)).then_inc(weights_in, 16)
                    else:
                        sp.dma_start(router_bias[:], everywhere(a["L0_ffn_br"], E)).then_inc(router_in, 16)
                    sp.dma_start(w1[:], a[names["w1"]].rearrange("e d f -> d e f")).then_inc(weights_in, 16)
                    sp.dma_start(w2[:], a[names["w2"]].rearrange("e (c p) d -> p e c d", p=P)).then_inc(weights_in, 16)
                    sp.dma_start(b2[:].rearrange("p e d -> p (e d)"), everywhere(a[names["b2"]].rearrange("e d -> (e d)"), E * D)).then_inc(weights_in, 16)
                    for c in range(FC):
                        sp.dma_start(b1[:, c, :], a[names["b1"]][:, c * P:(c + 1) * P].rearrange("e p -> p e"),
                                     allow_slow_non_contiguous=True).then_inc(weights_in, 16)

                @block.scalar
                def _(act):
                    act.nop().then_inc(rows_kept, 2)
                    with act.Fori(0, B // 2) as it:
                        for s in range(2):
                            b = it * 2 + s
                            act.wait_ge(normT_ready, b + 1)
                            act.wait_ge(logits_ready, b + 1)
                            act.activation(normT[:, s, :], psT[:, s, :], ACT.Copy).then_inc(normT_copied, 1)
                            act.activation(normed[:, ds(b * TB, TB), 0:D], norm.rows[:, s], ACT.Copy).then_inc(rows_kept, 1)
                    if last:
                        act.wait_ge(peaks_apart, 1)
                        act.activation(share[:, 1, :], share[:, 0, :], ACT.Exp).then_inc(gates_exped, 1)

                @block.gpsimd
                def _(pool):
                    norm.roots(pool, K)
                    pool.wait_ge(rows_kept, B + 2)
                    for k in range(top):
                        pool.wait_ge(slots_ready, k + 1)
                        pool.wait_ge(tagged, 2 * (k + 1))
                        for g in range(G):
                            pool.indirect_dma_start(K.routed_dram[top], bass.IndirectOffsetOnAxis(ap=slots[:, k, g:g + 1], axis=0),
                                                    normed[:, g, :], None).then_inc(routed, 16)
                    pool.wait_ge(routed, 16 * top * G)

                @block.tensor
                def _(pe):
                    pe.wait_ge(router_in, 16 if last else 32)
                    pe.nop().then_inc(logits_ready, 2)

                    def turn_rows(b, s):
                        pe.wait_ge(norm_ready, b + 1)
                        pe.wait_ge(rows_kept, b + 1)
                        for i in range(TB):
                            mm = pe.transpose(psT[:, s, i * P:(i + 1) * P], norm.rows[:, s, i, :], ident)
                        mm.then_inc(normT_ready, 1)

                    def rate(b, s):
                        pe.wait_ge(normT_copied, b + 1)
                        for i in range(TB):
                            mm = pe.matmul(psR[:, ds(b * (TB * E) + i * E, E)], normT[:, s, i * P:(i + 1) * P], router[:], start=True, stop=True,
                                           skip_group_check=True)
                        mm.then_inc(logits_ready, 1)

                    turn_rows(0, 0)
                    turn_rows(1, 1)
                    rate(0, 0)
                    with pe.Fori(1, B // 2) as it:
                        for s in range(2):
                            turn_rows(it * 2 + s, s)
                            rate(it * 2 + s - 1, 1 - s)
                    rate(B - 1, 1)
                    pe.wait_ge(picks_ready, 1)
                    pe.matmul(psC[:, 0:G * E], before[:], picks[:].rearrange("p g e -> p (g e)"), start=True, stop=False, skip_group_check=True)
                    for g in range(G - 1):
                        pe.matmul(psC[:, (g + 1) * E:G * E].rearrange("p (g e) -> p g e", e=E), all_ones[:],
                                  picks[:, g:g + 1, :].to_broadcast([P, G - 1 - g, E]), start=False, stop=(g == G - 2), skip_group_check=True)
                    for g in range(G):
                        mm = pe.matmul(psN[:, 0:E], all_ones[:], picks[:, g, :], start=(g == 0), stop=(g == G - 1))
                    mm.then_inc(ranks_ready, 1)

                @block.vector
                def _(dve):
                    if last:
                        dve.memset(router_bias[:], 0.0).then_inc(bias_set, 1)
                        dve.wait_ge(bias_set, 1)
                    norm.statistics(dve, K.hidden)
                    dve.wait_ge(norm.root_ready, 1)
                    with dve.Fori(0, B // 2) as it:
                        for s in range(2):
                            norm.batch(dve, it * 2 + s, s, K.hidden, rows_kept, norm_ready)
                    steps = Steps(dve, route_steps)
                    dve.wait_ge(router_in, 16 if last else 32)
                    dve.wait_ge(logits_ready, B + 2)
                    steps.then(dve.tensor_tensor(logits[:], psR[:, 0:G * E].rearrange("p (g e) -> p g e", e=E),
                                                 router_bias[:, None, :].to_broadcast([P, G, E]), ALU.add))

                    def per_tile(ap):
                        return ap[:, :, None].to_broadcast([P, G, E])

                    scores = logits
                    for k in range(top):
                        steps.then(dve.tensor_reduce(peak[:, k, :], scores[:], X, ALU.max))
                        steps.then(dve.tensor_tensor(equal[:], scores[:], per_tile(peak[:, k, :]), ALU.is_equal))
                        steps.then(dve.tensor_tensor(equal[:], equal[:], K.const("descend")[:, None, :].to_broadcast([P, G, E]), ALU.mult))
                        steps.then(dve.tensor_reduce(place[:], equal[:], X, ALU.max))
                        steps.then(dve.tensor_tensor(picked[k][:], equal[:], per_tile(place[:]), ALU.is_equal))
                        if k < top - 1:
                            steps.then(dve.scalar_tensor_tensor(work[:], picked[k][:], -BIG, logits[:], ALU.mult, ALU.add))
                            scores = work
                    if last:
                        dve.tensor_tensor(share[:, 0, :], peak[:, 1, :], peak[:, 0, :], ALU.subtract).then_inc(peaks_apart, 1)
                    steps.mark(dve.tensor_copy(before[:], K.const("before")))
                    steps.mark(dve.memset(all_ones[:], 1.0))
                    steps.wait()
                    if last:
                        dve.tensor_tensor(picks[:], picked[0][:], picked[1][:], ALU.add).then_inc(picks_ready, 1)
                        dve.wait_ge(gates_exped, 1)
                        steps.then(dve.tensor_scalar(place[:], share[:, 1, :], 1.0, None, ALU.add))
                        steps.then(dve.reciprocal(share[:, 0, :], place[:]))
                        steps.then(dve.tensor_tensor(share[:, 1, :], share[:, 1, :], share[:, 0, :], ALU.mult))
                    else:
                        dve.tensor_copy(picks[:], picked[0][:]).then_inc(picks_ready, 1)
                    dve.wait_ge(ranks_ready, 1)
                    steps.then(dve.tensor_tensor(many[:], psN[:, 0:E, None].to_broadcast([P, E, G]),
                                                 K.const("tiles128")[:, None, :].to_broadcast([P, E, G]), ALU.is_gt))
                    steps.then(dve.tensor_reduce(count[:], many[:], X, ALU.add))
                    steps.then(dve.tensor_tensor(pairs[:], count[:, None, :].to_broadcast([P, E, E]),
                                                 K.const("earlier").rearrange("p (e f) -> p e f", e=E), ALU.mult))
                    steps.then(dve.tensor_reduce(first[:], pairs[:], X, ALU.add))
                    steps.then(dve.tensor_tensor(end[:], first[:], count[:], ALU.add))
                    steps.then(dve.tensor_scalar(first[:], first[:], float(P), None, ALU.mult))
                    steps.then(dve.tensor_tensor(work[:], psC[:, 0:G * E].rearrange("p (g e) -> p g e", e=E),
                                                 first[:, None, :].to_broadcast([P, G, E]), ALU.add))

                    def tag(k):
                        dve.tensor_scalar(normed[:, :, D].bitcast(U32), K.const("token"), float(SPARE + k * N), None, ALU.add).then_inc(tagged, 1)
                        if last:
                            dve.tensor_copy(normed[:, :, D + 1], share[:, k, :]).then_inc(tagged, 1)
                        else:
                            dve.memset(normed[:, :, D + 1], 1.0).then_inc(tagged, 1)

                    tag(0)
                    for k in range(top):
                        steps.then(dve.tensor_tensor(equal[:], picked[k][:], work[:], ALU.mult))
                        steps.then(dve.tensor_reduce(place[:], equal[:], X, ALU.add))
                        dve.tensor_copy(slots[:, k, :], place[:]).then_inc(slots_ready, 1)
                        dve.wait_ge(slots_ready, k + 1)
                    steps.then(dve.tensor_tensor(passed[:], K.const("slot")[0:1, 0:tiles, None].to_broadcast([1, tiles, E]),
                                                 end[0:1, None, :].to_broadcast([1, tiles, E]), ALU.is_ge))
                    steps.then(dve.tensor_reduce(tile_expert[:], passed[:], X, ALU.add))
                    steps.then(dve.tensor_scalar(tile_expert[:], tile_expert[:], float(E - 1), None, ALU.min))
                    steps.then(dve.tensor_copy(owner[:], tile_expert[:]))
                    for k in range(1, top):
                        dve.wait_ge(routed, 16 * G * k)
                        tag(k)

        with ExitStack() as inner:
            sbe, pse, _ = allocators(nc, inner, phase + "mix")
            RING, PAIR = 8, 2
            assert RING <= E
            rows = sbe("rows", [P, RING, RW])
            rowsT = sbe("rowsT", [P, 2, P])
            hid = sbe("hid", [P, 2, F])
            hidT = sbe("hidT", [P, 2, F])
            result = sbe("result", [P, RING, D])
            stats, mv = sbe("stats", [P, 6]), sbe("mv", [P, 2, 2])
            square, root, pause = sbe("square", [P, 2]), sbe("root", [P, 2]), sbe("pause", [P, 1])
            psX = pse("psX", [P, 512])
            psH, psF, psY = pse("psH", [P, 2, F]), pse("psF", [P, 2, F]), pse("psY", [P, 2, 512])
            rows_in = [sem(f"rows_in{i}") for i in range(RING // PAIR)]
            result_out = [sem(f"result_out{i}") for i in range(RING // PAIR)]
            rowsT_ready, rowsT_copied = sem("rowsT_ready"), sem("rowsT_copied")
            hid_ready, hid_copied, hidT_ready, hidT_done = sem("hid_ready"), sem("hid_copied"), sem("hidT_ready"), sem("hidT_done")
            mixed_ready, result_ready, mix_steps = sem("mixed_ready"), sem("result_ready"), sem("mix_steps")
            square_ready, root_ready, paused = sem("mix_square_ready"), sem("mix_root_ready"), sem("paused")
            turns = tiles // RING
            MARKS = 6 if last else 0

            def slot_rows(ap, t):
                return ap[ds(t * P, PAIR * P), :].rearrange("(n p) d -> p n d", p=P)

            def expert(engine, t):
                return engine.value_load(owner[0:1, ds(t, 1)], min_val=0, max_val=E - 1)

            def experts(engine, first, n):
                _, values = nc.values_load_multi_w_load_instructions(owner[0:1, ds(first, n)], engines=(engine.engine,),
                                                                     min_val=0, max_val=E - 1)
                return list(values)

            with nc.Block() as block:
                @block.sync
                def _(sp):
                    def load(t, s):
                        sp.dma_start(rows[:, s:s + PAIR, :], slot_rows(K.routed_dram[top], t)).then_inc(rows_in[s // PAIR], 16)

                    for s in range(0, RING, PAIR):
                        load(s, s)
                    with sp.Fori(1, turns) as it:
                        for s in range(0, RING, PAIR):
                            sp.wait_ge(result_out[s // PAIR], it * (16 * PAIR))
                            load(it * RING + s, s)

                @block.gpsimd
                def _(pool):
                    def send(t, s):
                        pool.indirect_dma_start(K.result_dram[top], bass.IndirectOffsetOnAxis(ap=rows[:, s, D:D + 1].bitcast(U32), axis=0),
                                                result[:, s, :], None).then_inc(result_out[s // PAIR], 16)

                    def step(t, s, behind=True):
                        if last:
                            pool.wait_ge(square_ready, t + 1)
                            if behind:
                                pool.wait_ge(result_ready, t)
                            inverse_root(pool, K, root[:, s % 2:s % 2 + 1], square[:, s % 2:s % 2 + 1]).then_inc(root_ready, 1)
                            if behind:
                                send(t - 1, (s - 1) % RING)
                        else:
                            if behind:
                                pool.wait_ge(paused, t)
                            pool.wait_ge(result_ready, t + 1)
                            pool.tensor_tensor(pause[:], K.const("minus_half"), K.const("minus_half"), ALU.add).then_inc(paused, 1)
                            send(t, s)

                    for s in range(RING):
                        step(s, s, s > 0)
                    with pool.Fori(1, turns) as it:
                        for s in range(RING):
                            step(it * RING + s, s)
                    if last:
                        pool.wait_ge(result_ready, tiles)
                        send(tiles - 1, RING - 1)
                    for n in range(RING // PAIR):
                        pool.wait_ge(result_out[n], 16 * PAIR * turns)

                @block.tensor
                def _(pe):
                    def first_product(t, s, e):
                        pe.matmul(psH[:, s % 2, :], rowsT[:, s % 2, :], w1[:].rearrange("p e f -> p (e f)")[:, ds(e * F, F)],
                                  start=True, stop=True).then_inc(hid_ready, 1)

                    def turn_rows(s, turn):
                        pe.wait_ge(rows_in[s // PAIR], (turn + 1) * 16)
                        pe.transpose(psX[:, 0:P], rows[:, s, 0:D], ident).then_inc(rowsT_ready, 1)

                    def turn_hidden(t, s):
                        pe.wait_ge(hid_copied, t + 1)
                        for c in range(FC):
                            mm = pe.transpose(psF[:, s % 2, c * P:(c + 1) * P], hid[:, s % 2, c * P:(c + 1) * P], ident)
                        mm.then_inc(hidT_ready, 1)

                    def second_product(t, s, e, bank_used):
                        pe.wait_ge(hidT_done, t + 1)
                        if bank_used:
                            pe.wait_ge(result_ready, t - 1)
                        for c in range(FC):
                            mm = pe.matmul(psY[:, s % 2, 0:D], hidT[:, s % 2, c * P:(c + 1) * P],
                                           w2[:].rearrange("p e c d -> p (e c d)")[:, ds(e * (FC * D) + c * D, D)],
                                           start=(c == 0), stop=(c == FC - 1))
                        mm.then_inc(mixed_ready, 1)

                    def turn(first, it, opening, closing):
                        begin = 0 if opening else -2
                        e = dict(zip(range(begin, RING), experts(pe, first + begin, RING - begin)))
                        for s in range(RING):
                            t = first + s
                            pe.wait_ge(rowsT_copied, t + 1)
                            if s < RING - 1:
                                turn_rows(s + 1, it)
                            elif not closing:
                                turn_rows(0, it + 1)
                            first_product(t, s, e[s])
                            if s >= 1 or not opening:
                                turn_hidden(t - 1, (s + 1) % 2)
                            if s >= 2 or not opening:
                                second_product(t - 2, s % 2, e[s - 2], s >= 4 or not opening)
                        return e

                    pe.wait_ge(weights_in, weights_landed)
                    turn_rows(0, 0)
                    turn(0, 0, True, False)
                    with pe.Fori(1, turns - 1) as it:
                        turn(it * RING, it, False, False)
                    e = turn((turns - 1) * RING, turns - 1, False, True)
                    turn_hidden(tiles - 1, 1)
                    second_product(tiles - 2, 0, e[RING - 2], True)
                    second_product(tiles - 1, 1, e[RING - 1], True)

                @block.scalar
                def _(act):
                    def rows_copy(t, s):
                        act.wait_ge(rowsT_ready, t + 1)
                        act.activation(rowsT[:, s % 2, :], psX[:, 0:P], ACT.Copy).then_inc(rowsT_copied, 1)

                    def activate(t, s, e):
                        act.wait_ge(hidT_ready, t + 1)
                        flat = b1[:].rearrange("p c e -> p (c e)")
                        for c in range(FC):
                            ins = act.activation(hidT[:, s % 2, c * P:(c + 1) * P], psF[:, s % 2, c * P:(c + 1) * P], ACT.Relu,
                                                 bias=flat[:, ds(e + c * E, 1)])
                        ins.then_inc(hidT_done, 1)

                    act.wait_ge(weights_in, weights_landed)
                    e = experts(act, 0, RING - 2)
                    rows_copy(0, 0)
                    rows_copy(1, 1)
                    for s in range(2, RING):
                        rows_copy(s, s)
                        activate(s - 2, s, e[s - 2])
                    with act.Fori(1, turns) as it:
                        e = experts(act, it * RING - 2, RING)
                        for s in range(RING):
                            rows_copy(it * RING + s, s)
                            activate(it * RING + s - 2, s, e[s])
                    e = experts(act, tiles - 2, 2)
                    activate(tiles - 2, 0, e[0])
                    activate(tiles - 1, 1, e[1])

                @block.vector
                def _(dve):
                    steps = Steps(dve, mix_steps)

                    def hidden_copy(t, s):
                        dve.wait_ge(hid_ready, t + 1)
                        dve.tensor_copy(hid[:, s % 2, :], psH[:, s % 2, :]).then_inc(hid_copied, 1)

                    def of_expert(table, e):
                        return table[:].rearrange("p e d -> p (e d)")[:, ds(e * D, D)]

                    def begin(t, s, it, e):
                        res, mixed = result[:, s, :], psY[:, s % 2, 0:D]
                        if not last:
                            dve.wait_ge(mixed_ready, t + 1)
                            dve.tensor_tensor(res, mixed, of_expert(b2, e), ALU.add).then_inc(result_ready, 1)
                            return
                        dve.wait_ge(rows_in[s // PAIR], 16 * it + 16)
                        steps.then(dve.tensor_tensor(res, rows[:, s, 0:D], of_expert(b2, e), ALU.add))
                        dve.wait_ge(mixed_ready, t + 1)
                        steps.then(dve.tensor_tensor(res, mixed, res, ALU.add))
                        steps.mark(dve.bn_stats(stats[:], res))
                        steps.wait_apart(pause[:])
                        steps.then(dve.bn_aggr(mv[:, s % 2, :], stats[:]))
                        dve.tensor_scalar(square[:, s % 2:s % 2 + 1], mv[:, s % 2, 1:2], RMS_EPS, None, ALU.add).then_inc(square_ready, 1)

                    def finish(t, s, e):
                        if not last:
                            return
                        res = result[:, s, :]
                        steps.then(dve.scalar_tensor_tensor(res, res, mv[:, s % 2, 0:1], of_expert(gamma, e), ALU.subtract, ALU.mult))
                        dve.wait_ge(root_ready, t + 1)
                        steps.then(dve.scalar_tensor_tensor(res, res, root[:, s % 2:s % 2 + 1], of_expert(beta, e), ALU.mult, ALU.add))
                        dve.tensor_scalar(res, res, rows[:, s, D + 1:D + 2], None, ALU.mult).then_inc(result_ready, 1)

                    dve.wait_ge(weights_in, weights_landed)
                    e = experts(dve, 0, RING - 2)
                    hidden_copy(0, 0)
                    hidden_copy(1, 1)
                    for s in range(2, RING):
                        hidden_copy(s, s)
                        begin(s - 2, s - 2, 0, e[s - 2])
                        if s > 2:
                            finish(s - 3, s - 3, e[s - 3])
                    with dve.Fori(1, turns) as it:
                        steps.turn(it - 1, RING * MARKS)
                        e = experts(dve, it * RING - 3, RING + 1)
                        for s in range(RING):
                            t = it * RING + s
                            hidden_copy(t, s)
                            begin(t - 2, (s - 2) % RING, it - 1 if s < 2 else it, e[s + 1])
                            finish(t - 3, (s - 3) % RING, e[s])
                    steps.end(turns - 1)
                    e = experts(dve, tiles - 3, 3)
                    begin(tiles - 2, RING - 2, turns - 1, e[1])
                    finish(tiles - 3, RING - 3, e[0])
                    begin(tiles - 1, RING - 1, turns - 1, e[2])
                    finish(tiles - 2, RING - 2, e[1])
                    finish(tiles - 1, RING - 1, e[2])

        with ExitStack() as inner:
            sbb, _, _ = allocators(nc, inner, phase + "back")
            back = sbb("back", [P, top, G, D])
            back_in, added, stored = [sem(f"back_in{q}") for q in range(4)], sem("added"), sem("stored")
            QT = G // 4
            with nc.Block() as block:
                @block.sync
                def _(sp):
                    for q in range(4):
                        part = slice(q * QT, (q + 1) * QT)
                        for k in range(top):
                            tokens = K.result_dram[top][SPARE + k * N:SPARE + (k + 1) * N, :].rearrange("(g p) d -> p g d", p=P)
                            sp.dma_start(back[:, k, part, :], tokens[:, part, :]).then_inc(back_in[q], 16)
                    if last:
                        rows_out = out.rearrange("b (i p) d -> p (b i) d", p=P)
                        for q in range(4):
                            part = slice(q * QT, (q + 1) * QT)
                            sp.wait_ge(added, top * (q + 1))
                            sp.dma_start(rows_out[:, part, :], K.hidden[:, part, :]).then_inc(stored, 16)
                        sp.wait_ge(stored, 64)

                @block.vector
                def _(dve):
                    for q in range(4):
                        part = slice(q * QT, (q + 1) * QT)
                        dve.wait_ge(back_in[q], 16 * top)
                        for k in range(top):
                            rows = K.hidden[:, part, :]
                            dve.tensor_tensor(rows, rows, back[:, k, part, :], ALU.add).then_inc(added, 1)
                            dve.wait_ge(added, q * top + k + 1)


def cross_attention(nc, a, K):
    with ExitStack() as ctx:
        sb, ps, sem = allocators(nc, ctx, "cross")
        ident = K.const("ident")
        qT = sb("normT", [P, (B + 1) * L])
        mixedT = sb("mixedT", [P, B * L])
        head_sums = (qT, mixedT)
        norm_ready, normT_ready, normT_copied = sem("norm_ready"), sem("normT_ready"), sem("normT_copied")

        with ExitStack() as inner:
            sbn, psn, _ = allocators(nc, inner, "crossnorm")
            norm = LayerNorm(nc, inner, "crossnorm")
            psT = psn("psT", [P, 2, L])
            tail_set = sem("tail_set")
            with nc.Block() as block:
                @block.vector
                def _(dve):
                    dve.memset(qT[:, B * L:(B + 1) * L], 0.0).then_inc(tail_set, 1)
                    norm.statistics(dve, K.hidden)
                    dve.wait_ge(norm.root_ready, 1)
                    with dve.Fori(0, B // 2) as it:
                        for s in range(2):
                            norm.batch(dve, it * 2 + s, s, K.hidden, normT_copied, norm_ready)

                @block.gpsimd
                def _(pool):
                    norm.roots(pool, K)

                @block.tensor
                def _(pe):
                    with pe.Fori(0, B // 2) as it:
                        for s in range(2):
                            b = it * 2 + s
                            pe.wait_ge(norm_ready, b + 1)
                            pe.wait_ge(normT_copied, b + 1)
                            for i in range(TB):
                                mm = pe.transpose(psT[:, s, i * P:(i + 1) * P], norm.rows[:, s, i, :], ident)
                            mm.then_inc(normT_ready, 1)

                @block.scalar
                def _(act):
                    act.nop().then_inc(normT_copied, 2)
                    with act.Fori(0, B // 2) as it:
                        for s in range(2):
                            b = it * 2 + s
                            act.wait_ge(normT_ready, b + 1)
                            act.activation(qT[:, ds(b * L, L)], psT[:, s, :], ACT.Copy).then_inc(normT_copied, 1)

        with ExitStack() as inner:
            sba, psa, _ = allocators(nc, inner, "attend")
            q_high = [sba(f"q_high{h}", [P, L], F32R) for h in range(H1)]
            q_low = [sba(f"q_low{h}", [P, L], F32R) for h in range(H1)]
            maxima = sba("maxima", [P, TB, VC], F32R)
            WR = 2 * TB
            weights = sba("weights", [P, WR, KC])
            sums, scales = sba("sums", [P, WR, VC]), sba("scales", [P, WR, VC])
            highT, lowT = sba("highT", [P, 2, 2, KC], F32R), sba("lowT", [P, 2, 2, KC], F32R)
            chunk_values = sba("chunk_values", [P, 2, SUB, 2, DH1], F32R)
            zero = sba("zero", [1, L])
            psL, psT = psa("psL", [P, TB, KC]), psa("psT", [P, 2, KC])
            psA = psa("psA", [P, L])
            psQ = psa("psQ", [P, L])
            zero_set, q_ready, q_highs, q_lows = sem("zero_set"), sem("q_ready"), sem("q_highs"), sem("q_lows")
            logits_ready, maxima_ready, shifted, exped = sem("logits_ready"), sem("maxima_ready"), sem("shifted"), sem("exped")
            summed, scales_ready, normalised = sem("summed"), sem("scales_ready"), sem("normalised")
            left_turned, right_turned, highs, right_reduced, left_lows, right_lows = (sem(n) for n in (
                "left_turned", "right_turned", "highs", "right_reduced", "left_lows", "right_lows"))
            value_highs, value_lows, pairs_mixed = sem("value_highs"), sem("value_lows"), sem("pairs_mixed")
            run_ready, run_copied = sem("run_ready"), sem("run_copied")
            LEFT, RIGHT = 0, 1
            AHEAD = 6

            def runs(engine, run):
                with engine.Fori(0, B) as b:
                    for h in range(H1):
                        run(b, h)

            def unit(b, h, c):
                return ((b * H1 + h) * NKC + c) * TB

            def pair(b, h, c):
                return ((b * H1 + h) * NKC + c) * 2

            def chunks(engine, b, h, chunk):
                chunk(0, 0)
                with engine.Fori(0, (NKC - 4) // 2) as i:
                    chunk(i * 2 + 1, 1)
                    chunk(i * 2 + 2, 0)
                for c in range(NKC - 3, NKC):
                    chunk(c, c % 2)

            def videos(ap):
                return ap.rearrange("p (v f) -> p v f", f=FR)

            with nc.Block() as block:
                @block.tensor
                def _(pe):
                    def project(h, cols):
                        pe.matmul(psQ[:], K.wq2[:, h, :], qT[:, cols], start=True, stop=True).then_inc(q_ready, 1)

                    def logits(h, s, key):
                        tile = slice(s * P, (s + 1) * P)
                        pe.matmul(psL[:, s, :], q_high[h][:, tile], K.keys[:, ds(key, KC)], start=True, stop=False, skip_group_check=True)
                        pe.matmul(psL[:, s, :], q_low[h][:, tile], K.keys[:, ds(key, KC)], start=False, stop=False,
                                  skip_group_check=True).then_inc(logits_ready, 1)

                    def shift(s):
                        pe.matmul(videos(psL[:, s, :]), K.neg_ident[:], maxima[:, s, :, None].to_broadcast([P, VC, FR]),
                                  start=False, stop=True, skip_group_check=True).then_inc(shifted, 1)

                    def turn_weights(w, side):
                        for t in range(2):
                            for k in (2 * side, 2 * side + 1):
                                at = (k % 2) * 2 * P + t * P
                                mm = pe.matmul(psT[:, side, at:at + P], weights[:, w + t, k * P:(k + 1) * P], ident, is_transpose=True,
                                               start=(at == 0), stop=False, skip_group_check=True)
                        return mm

                    def mix(j, half, parity, side):
                        for k in (2 * side, 2 * side + 1):
                            at = slice((k % 2) * 2 * P, (k % 2 + 1) * 2 * P)
                            value = chunk_values[:, parity, k].rearrange("p a e -> p (a e)")
                            for part in (highT, lowT):
                                mm = pe.matmul(psA[:, j * 2 * P:(j + 1) * 2 * P], value, part[:, half, side, at],
                                               start=False, stop=(k == SUB - 1), skip_group_check=True)
                        return mm

                    def pair_step(u, n, j, parity, head, key, begins, earlier):
                        w, newest = 4 * parity + 2 * j, (2 * j + AHEAD) % TB
                        pe.wait_ge(exped, u + AHEAD - 3)
                        logits(head, newest, key)
                        pe.wait_ge(normalised, u + 2)
                        pe.wait_ge(left_lows, n + 1)
                        turn_weights(w, LEFT).then_inc(left_turned, 1)
                        pe.wait_ge(right_lows, n + 1)
                        turn_weights(w, RIGHT).then_inc(right_turned, 1)
                        pe.wait_ge(maxima_ready, u + AHEAD)
                        shift((newest + 3) % TB)
                        if begins:
                            begins()
                        if earlier:
                            mix(*earlier, LEFT)
                            mix(*earlier, RIGHT).then_inc(pairs_mixed, 1)
                        pe.wait_ge(highs, 2 * n + 2)
                        pe.matmul(psT[:, RIGHT, :], K.neg_ident[:], highT[:, j, RIGHT, :], start=False, stop=True,
                                  skip_group_check=True).then_inc(right_reduced, 1)
                        pe.wait_ge(maxima_ready, u + AHEAD + 1)
                        shift(newest)
                        pe.wait_ge(exped, u + AHEAD - 2)
                        logits(head, newest + 1, key)

                    pe.nop().then_inc(pairs_mixed, 4)
                    pe.wait_ge(zero_set, 1)
                    project(0, slice(0, L))
                    pe.wait_ge(q_highs, 1)
                    pe.wait_ge(q_lows, 1)
                    for u in range(AHEAD):
                        if u >= 1:
                            pe.wait_ge(maxima_ready, u)
                            shift((u - 1) % TB)
                        if u >= TB:
                            pe.wait_ge(exped, u - 3)
                        logits(0, u % TB, u // TB * KC)

                    def run(b, h):
                        def begin():
                            project(1 - h, ds((b + h) * L, L))
                            pe.wait_ge(run_copied, b * H1 + h + 1)
                            pe.matmul(psA[:], zero[0:1, 0:P], zero[:], start=True, stop=False, skip_group_check=True)

                        def chunk(c, parity):
                            u, n = unit(b, h, c), pair(b, h, c)
                            at_end = isinstance(c, int)
                            first = at_end and c == 0

                            def target(ahead):
                                if at_end and c + ahead >= NKC:
                                    return 1 - h, (1 - h) * KEYS + (c + ahead - NKC) * KC
                                return h, h * KEYS + (c + ahead) * KC

                            pair_step(u, n, 0, parity, *target(1), begin if first else None, None if first else (1, 1, 1 - parity))
                            pe.wait_ge(value_lows, (b * H1 + h) * NKC + c + 1)
                            if at_end and c == NKC - 2:
                                pe.wait_ge(q_highs, b * H1 + h + 2)
                                pe.wait_ge(q_lows, b * H1 + h + 2)
                            pair_step(u + 2, n + 1, 1, parity, *target(2), None, (0, 0, parity))

                        chunks(pe, b, h, chunk)
                        pe.wait_ge(left_lows, pair(b, h, NKC) + 1)
                        pe.wait_ge(right_lows, pair(b, h, NKC) + 1)
                        mix(1, 1, 1, LEFT)
                        mm = mix(1, 1, 1, RIGHT)
                        mm.then_inc(pairs_mixed, 1)
                        pe.wait_ge(pairs_mixed, pair(b, h, NKC) + 4)
                        pe.nop().then_inc(run_ready, 1)

                    runs(pe, run)

                @block.vector
                def _(dve):
                    dve.memset(zero[:], 0.0).then_inc(zero_set, 1)

                    def low(h, n):
                        dve.wait_ge(q_highs, n)
                        dve.scalar_tensor_tensor(q_low[h][:], psQ[:], K.bq2[:, h:h + 1], q_high[h][:].bitcast(F32),
                                                 ALU.add, ALU.subtract).then_inc(q_lows, 1)

                    def maximum(s, u):
                        dve.wait_ge(logits_ready, u + 1)
                        dve.tensor_reduce(maxima[:, s, :], videos(psL[:, s, :]), X, ALU.max).then_inc(maxima_ready, 1)

                    def total(w, u):
                        dve.wait_ge(exped, u + 1)
                        dve.tensor_reduce(sums[:, w, :], videos(weights[:, w, :]), X, ALU.add).then_inc(summed, 1)

                    def reciprocal(w, u):
                        dve.wait_ge(summed, u + 1)
                        dve.reciprocal(scales[:, w, :], sums[:, w, :]).then_inc(scales_ready, 1)

                    def left_low(n, half):
                        dve.wait_ge(highs, 2 * n + 1)
                        dve.tensor_tensor(lowT[:, half, LEFT, :], psT[:, LEFT, :], highT[:, half, LEFT, :].bitcast(F32),
                                          ALU.subtract).then_inc(left_lows, 1)

                    def step(u, w, between=None):
                        maximum((w + AHEAD) % TB, u + AHEAD)
                        if between:
                            left_low(*between)
                        reciprocal((w + AHEAD - 2) % WR, u + AHEAD - 2)
                        total((w + AHEAD - 1) % WR, u + AHEAD - 1)

                    dve.nop().then_inc(left_lows, 1)
                    low(0, 1)
                    for u in range(AHEAD):
                        maximum(u % TB, u)
                        if u >= 2:
                            reciprocal(u - 2, u - 2)
                        if u >= 1:
                            total(u - 1, u - 1)

                    def run(b, h):
                        def chunk(c, parity):
                            u, n = unit(b, h, c), pair(b, h, c)
                            for j in range(2):
                                step(u + 2 * j, 4 * parity + 2 * j, (n + j, j))
                                if isinstance(c, int) and c == 0 and j == 0:
                                    low(1 - h, b * H1 + h + 2)
                                step(u + 2 * j + 1, 4 * parity + 2 * j + 1)

                        chunks(dve, b, h, chunk)

                    runs(dve, run)

                @block.scalar
                def _(act):
                    def high(h, n):
                        act.wait_ge(q_ready, n)
                        act.activation(q_high[h][:], psQ[:], ACT.Identity, bias=K.bq2[:, h:h + 1]).then_inc(q_highs, 1)

                    def exponential(w, u):
                        act.wait_ge(shifted, u + 1)
                        act.activation(weights[:, w, :], psL[:, w % TB, :], ACT.Exp, scale=float(DH1) ** -0.5).then_inc(exped, 1)

                    def high_half(n, half, side, turned):
                        act.wait_ge(turned, n + 1)
                        act.activation(highT[:, half, side, :], psT[:, side, :], ACT.Copy).then_inc(highs, 1)

                    def right_low(n, half):
                        act.wait_ge(right_reduced, n + 1)
                        act.activation(lowT[:, half, RIGHT, :], psT[:, RIGHT, :], ACT.Copy).then_inc(right_lows, 1)

                    act.nop().then_inc(right_lows, 1)
                    act.nop().then_inc(run_copied, 1)
                    high(0, 1)
                    for u in range(AHEAD - 1):
                        exponential(u, u)

                    def run(b, h):
                        def chunk(c, parity):
                            u, n = unit(b, h, c), pair(b, h, c)
                            for j in range(2):
                                w = 4 * parity + 2 * j + AHEAD
                                high_half(n + j, j, LEFT, left_turned)
                                high_half(n + j, j, RIGHT, right_turned)
                                exponential((w - 1) % WR, u + 2 * j + AHEAD - 1)
                                if isinstance(c, int) and c == 0 and j == 0:
                                    high(1 - h, b * H1 + h + 2)
                                right_low(n + j, j)
                                exponential(w % WR, u + 2 * j + AHEAD)

                        chunks(act, b, h, chunk)
                        act.wait_ge(run_ready, b * H1 + h + 1)
                        act.activation(head_sums[h][:, ds(b * L, L)].rearrange("p (side r) -> p side r", side=2),
                                       psA[:].rearrange("p (r side) -> p side r", side=2), ACT.Copy,
                                       scale=1.0 / VID).then_inc(run_copied, 1)

                    runs(act, run)

                @block.gpsimd
                def _(pool):
                    def normalise(u, s):
                        pool.wait_ge(scales_ready, u + 1)
                        w = videos(weights[:, s, :])
                        pool.tensor_tensor(w, w, scales[:, s, :, None].to_broadcast([P, VC, FR]), ALU.mult).then_inc(normalised, 1)

                    def run(b, h):
                        def chunk(c, parity):
                            m = (b * H1 + h) * NKC + c
                            value = K.values[:, h, ds(c * SUB, SUB), :]
                            pool.wait_ge(pairs_mixed, 2 * m + 2)
                            normalise(4 * m, 4 * parity)
                            pool.tensor_copy(chunk_values[:, parity, :, 0, :], value).then_inc(value_highs, 1)
                            pool.wait_ge(value_highs, m + 1)
                            normalise(4 * m + 1, 4 * parity + 1)
                            pool.tensor_tensor(chunk_values[:, parity, :, 1, :], value, chunk_values[:, parity, :, 0, :].bitcast(F32),
                                               ALU.subtract).then_inc(value_lows, 1)
                            normalise(4 * m + 2, 4 * parity + 2)
                            normalise(4 * m + 3, 4 * parity + 3)

                        chunks(pool, b, h, chunk)

                    runs(pool, run)

        with ExitStack() as inner:
            sbo, pso, _ = allocators(nc, inner, "crossout")
            psY = pso("psY", [P, 2, L])
            stage = sbo("stage", [P, 2, H1, 2, L // 2])
            bias_added, out_ready, out_added, staged = sem("bias_added"), sem("out_ready"), sem("out_added"), sem("staged")
            with nc.Block() as block:
                @block.gpsimd
                def _(pool):
                    with pool.Fori(0, B) as b:
                        rows = K.hidden[:, ds(b * TB, TB), :]
                        pool.tensor_tensor(rows, rows, K.bo_all[:, None, :].to_broadcast([P, TB, D]), ALU.add).then_inc(bias_added, 1)

                @block.scalar
                def _(act):
                    with act.Fori(0, B // 2) as it:
                        for s in range(2):
                            b = it * 2 + s
                            act.wait_ge(out_ready, b + 1)
                            for h in range(H1):
                                ins = act.activation(stage[:, s, h].rearrange("p side r -> p (side r)"), head_sums[h][:, ds(b * L, L)], ACT.Copy)
                            ins.then_inc(staged, 1)

                @block.tensor
                def _(pe):
                    pe.nop().then_inc(out_ready, 2)
                    with pe.Fori(0, B // 2) as it:
                        for s in range(2):
                            b = it * 2 + s
                            pe.wait_ge(staged, b + 1)
                            pe.wait_ge(out_added, b + 1)
                            for i in range(TB):
                                h, m = i // (TB // H1), i % (TB // H1)
                                for side in range(2):
                                    mm = pe.matmul(psY[:, s, i * D:(i + 1) * D], stage[:, s, h, side, m * P:(m + 1) * P], K.wo2[:, side, :],
                                                   start=(side == 0), stop=(side == 1), skip_group_check=True)
                            mm.then_inc(out_ready, 1)

                @block.vector
                def _(dve):
                    dve.nop().then_inc(out_added, 2)
                    with dve.Fori(0, B // 2) as it:
                        for s in range(2):
                            b = it * 2 + s
                            dve.wait_ge(bias_added, b + 1)
                            dve.wait_ge(out_ready, b + 3)
                            rows = K.hidden[:, ds(b * TB, TB), :].rearrange("p i d -> p (i d)")
                            dve.tensor_tensor(rows, rows, psY[:, s, :], ALU.add).then_inc(out_added, 1)


def audio_tower(nc, a, out):
    with ExitStack() as ctx:
        K = Kept(nc, ctx, a)
        select_and_project(nc, a, K)
        retention(nc, a, K)
        route_and_mix(nc, a, K, 1)
        cross_attention(nc, a, K)
        route_and_mix(nc, a, K, 2, out)


_OUT = ((B, L, D), "float32")


def kernel(**inputs):
    import numpy as _np
    import concourse.bacc as _bacc
    from concourse import mybir as _mybir
    from concourse.bass_utils import run_bass_kernel_spmd as _run

    nc = _bacc.Bacc("TRN2", target_bir_lowering=False, num_devices=1)
    arrays, aps = {}, {}
    for name, value in {**inputs, "shape_constants": CONSTANTS}.items():
        value = _np.ascontiguousarray(value)
        arrays[f"in_{name}_dram"] = value
        aps[name] = nc.dram_tensor(f"in_{name}_dram", value.shape, _mybir.dt.from_np(value.dtype), kind="ExternalInput").ap()
    out = nc.dram_tensor("out_0_dram", _OUT[0], _mybir.dt.from_np(_np.dtype(_OUT[1])), kind="ExternalOutput").ap()
    audio_tower(nc, aps, out)
    r = _run(nc, [arrays], core_ids=[0])
    return r.results[0]["out_0_dram"]
```
